# Optimizing a Trainium2 kernel written in Bass

```python
import numpy as np
import jax
import jax.numpy as jnp

def _softmax(x, axis=-1):
    return jax.nn.softmax(x, axis=axis)

def _gelu(x):
    return jax.nn.gelu(x, approximate=True)

def _silu(x):
    return jax.nn.silu(x)

def _sigmoid(x):
    return jax.nn.sigmoid(x)

def _layernorm(x, axis=-1, eps=1e-05):
    m = jnp.mean(x, axis=axis, keepdims=True)
    v = jnp.var(x, axis=axis, keepdims=True)
    return (x - m) / jnp.sqrt(v + eps)

def _scatter_add(tgt, idx, src, axis=0):
    return tgt.at[idx].add(src)

def _segment_sum(src, seg, n):
    return jax.ops.segment_sum(src, seg, n)
kernel_name = 'mk_gnn_preln_d4_gnn_r8_14fdbb'

def setup_inputs(seed: int=0):
    np.random.seed(seed)
    _w = jnp.asarray

    def _rec_inputs():
        import jax
        import jax.numpy as jnp
        _gk = jax.random.key(seed)
        x = -0.000202 + 1 * jax.random.normal(jax.random.fold_in(_gk, 1), (6250, 128), jnp.float32)
        _s = jax.random.randint(jax.random.fold_in(_gk, 2), (100000,), 0, 6250, jnp.int32)
        _d = jax.random.randint(jax.random.fold_in(_gk, 3), (100000,), 0, 6250, jnp.int32)
        _loop = jnp.arange(6250, dtype=jnp.int32)
        src = jnp.concatenate([_s, _d, _loop])
        dst = jnp.concatenate([_d, _s, _loop])
        _o = jnp.argsort(dst, stable=True)
        src = src[_o]
        dst = dst[_o]
        edge_weight = jax.random.uniform(jax.random.fold_in(_gk, 12), (206250,), jnp.float32, 0.0, 0.999998)
        return (x, src, dst, edge_weight)
    x, src, dst, edge_weight = _rec_inputs()

    def _L0_gnn_setup():
        import jax, jax.numpy as jnp
        import numpy as np
        N, C, E = (6250, 128, 75000)
        EPS = 1e-05
        SLOPE = 0.2

        def layer_norm(h, g, b):
            m = jnp.mean(h, axis=-1, keepdims=True)
            v = jnp.mean((h - m) ** 2, axis=-1, keepdims=True)
            return (h - m) * jax.lax.rsqrt(v + EPS) * g + b
        key = jax.random.key(seed)
        ks = jax.random.split(key, 12)
        s1 = 1.0 / np.sqrt(2 * C)
        s2 = 1.0 / np.sqrt(C)
        return {'x': jax.random.normal(ks[0], (N, C), dtype=jnp.float32), 'edge_index': jax.random.randint(ks[1], (2, E), 0, N, dtype=jnp.int64), 'edge_attr': jax.random.uniform(ks[2], (E,), dtype=jnp.float32), 'w1': jax.random.uniform(ks[3], (2 * C, C), jnp.float32, -s1, s1), 'b1': jax.random.uniform(ks[4], (C,), jnp.float32, -s1, s1), 'g1': jnp.ones((C,), jnp.float32), 'be1': jnp.zeros((C,), jnp.float32), 'w2': jax.random.uniform(ks[5], (C, C), jnp.float32, -s2, s2), 'b2': jax.random.uniform(ks[6], (C,), jnp.float32, -s2, s2), 'g2': jnp.ones((C,), jnp.float32), 'be2': jnp.zeros((C,), jnp.float32)}
    _L0_gnn_all = _L0_gnn_setup()
    _L0_gnn_in = {k: v for k, v in _L0_gnn_all.items() if k in ('w1', 'b1', 'g1', 'be1', 'w2', 'b2', 'g2', 'be2')}
    del _L0_gnn_all

    def _L1_gnn_setup():
        import jax, jax.numpy as jnp
        import numpy as np
        N_NODES = 6250
        N_EDGES = 100000
        D_FEAT = 128
        HIDDEN = 128
        OUT = 128

        def _sage_conv(x, src, dst, W_l, b_l, W_r, n_nodes):
            msgs = x[src]
            summed = jax.ops.segment_sum(msgs, dst, num_segments=n_nodes)
            cnt = jax.ops.segment_sum(jnp.ones((src.shape[0],), x.dtype), dst, num_segments=n_nodes)
            aggr = summed / jnp.maximum(cnt, 1.0)[:, None]
            return aggr @ W_l + b_l + x @ W_r
        key = jax.random.key(seed)
        ks = jax.random.split(key, 8)
        sc_in = 1.0 / np.sqrt(D_FEAT)
        sc_h = 1.0 / np.sqrt(HIDDEN)
        return {'x': jax.random.normal(ks[0], (N_NODES, D_FEAT), dtype=jnp.float32), 'edge_index': jax.random.randint(ks[1], (2, N_EDGES), 0, N_NODES, dtype=jnp.int64), 'W1_l': jax.random.normal(ks[2], (D_FEAT, HIDDEN), dtype=jnp.float32) * sc_in, 'b1_l': jnp.zeros((HIDDEN,), dtype=jnp.float32), 'W1_r': jax.random.normal(ks[3], (D_FEAT, HIDDEN), dtype=jnp.float32) * sc_in, 'W2_l': jax.random.normal(ks[4], (HIDDEN, OUT), dtype=jnp.float32) * sc_h, 'b2_l': jnp.zeros((OUT,), dtype=jnp.float32), 'W2_r': jax.random.normal(ks[5], (HIDDEN, OUT), dtype=jnp.float32) * sc_h}
    _L1_gnn_all = _L1_gnn_setup()
    _L1_gnn_in = {k: v for k, v in _L1_gnn_all.items() if k in ('W1_l', 'b1_l', 'W1_r', 'W2_l', 'b2_l', 'W2_r')}
    del _L1_gnn_all

    def _L2_gnn_setup():
        import jax, jax.numpy as jnp
        import numpy as np
        from jax.ops import segment_sum, segment_max
        N_NODES = 6250
        N_EDGES = 200000
        IN_DIM = 128
        OUT_DIM = 128
        N_HEADS = 4
        NEG_SLOPE = 0.2

        def _leaky(v):
            return jnp.where(v >= 0, v, NEG_SLOPE * v)
        key = jax.random.key(seed)
        ks = jax.random.split(key, 6)
        x = jax.random.normal(ks[0], (N_NODES, IN_DIM), dtype=jnp.float32)
        edge_index = jax.random.randint(ks[1], (2, N_EDGES), 0, N_NODES, dtype=jnp.int32)
        Wq = jax.random.normal(ks[2], (N_HEADS, IN_DIM), dtype=jnp.float32) * 0.1
        Wk = jax.random.normal(ks[3], (N_HEADS, IN_DIM), dtype=jnp.float32) * 0.1
        Wl = jax.random.normal(ks[4], (OUT_DIM, IN_DIM), dtype=jnp.float32) * 0.05
        bl = jax.random.normal(ks[5], (OUT_DIM,), dtype=jnp.float32) * 0.05
        return {'x': x, 'edge_index': edge_index, 'Wq': Wq, 'Wk': Wk, 'Wl': Wl, 'bl': bl}
    _L2_gnn_all = _L2_gnn_setup()
    _L2_gnn_in = {k: v for k, v in _L2_gnn_all.items() if k in ('Wq', 'Wk', 'Wl', 'bl')}
    del _L2_gnn_all

    def _L3_gnn_setup():
        import jax, jax.numpy as jnp
        import numpy as np
        N_NODES = 6250
        IN_C = 128
        OUT_C = 128
        N_EDGES = 100000
        key = jax.random.key(seed)
        k1, k2, k3, k4, k5 = jax.random.split(key, 5)
        x = jax.random.normal(k1, (N_NODES, IN_C), dtype=jnp.float32)
        HE = jax.random.randint(k2, (2, N_EDGES), 0, N_NODES, dtype=jnp.int64)
        HEW = jax.random.uniform(k3, (N_EDGES,), dtype=jnp.float32)
        limit = float(np.sqrt(6.0 / (IN_C + OUT_C)))
        W = jax.random.uniform(k4, (IN_C, OUT_C), dtype=jnp.float32, minval=-limit, maxval=limit)
        b = jnp.zeros((OUT_C,), dtype=jnp.float32)
        return {'x': x, 'HE': HE, 'HEW': HEW, 'W': W, 'b': b}
    _L3_gnn_all = _L3_gnn_setup()
    _L3_gnn_in = {k: v for k, v in _L3_gnn_all.items() if k in ('W', 'b')}
    del _L3_gnn_all
    return {'x': x, 'src': src, 'dst': dst, 'edge_weight': edge_weight, 'L0_gnn_w1': _L0_gnn_in['w1'], 'L0_gnn_b1': _L0_gnn_in['b1'], 'L0_gnn_g1': _L0_gnn_in['g1'], 'L0_gnn_be1': _L0_gnn_in['be1'], 'L0_gnn_w2': _L0_gnn_in['w2'], 'L0_gnn_b2': _L0_gnn_in['b2'], 'L0_gnn_g2': _L0_gnn_in['g2'], 'L0_gnn_be2': _L0_gnn_in['be2'], 'L1_gnn_W1_l': _L1_gnn_in['W1_l'], 'L1_gnn_b1_l': _L1_gnn_in['b1_l'], 'L1_gnn_W1_r': _L1_gnn_in['W1_r'], 'L1_gnn_W2_l': _L1_gnn_in['W2_l'], 'L1_gnn_b2_l': _L1_gnn_in['b2_l'], 'L1_gnn_W2_r': _L1_gnn_in['W2_r'], 'L2_gnn_Wq': _L2_gnn_in['Wq'], 'L2_gnn_Wk': _L2_gnn_in['Wk'], 'L2_gnn_Wl': _L2_gnn_in['Wl'], 'L2_gnn_bl': _L2_gnn_in['bl'], 'L3_gnn_W': _L3_gnn_in['W'], 'L3_gnn_b': _L3_gnn_in['b']}

def reference(x, src, dst, edge_weight, L0_gnn_w1, L0_gnn_b1, L0_gnn_g1, L0_gnn_be1, L0_gnn_w2, L0_gnn_b2, L0_gnn_g2, L0_gnn_be2, L1_gnn_W1_l, L1_gnn_b1_l, L1_gnn_W1_r, L1_gnn_W2_l, L1_gnn_b2_l, L1_gnn_W2_r, L2_gnn_Wq, L2_gnn_Wk, L2_gnn_Wl, L2_gnn_bl, L3_gnn_W, L3_gnn_b):
    import jax
    import jax.numpy as jnp

    def _L0_gnn_ref(x, edge_index, edge_attr, w1, b1, g1, be1, w2, b2, g2, be2):
        import jax, jax.numpy as jnp
        import numpy as np
        N, C, E = (6250, 128, 75000)
        EPS = 1e-05
        SLOPE = 0.2

        def layer_norm(h, g, b):
            m = jnp.mean(h, axis=-1, keepdims=True)
            v = jnp.mean((h - m) ** 2, axis=-1, keepdims=True)
            return (h - m) * jax.lax.rsqrt(v + EPS) * g + b
        source, target = (edge_index[0], edge_index[1])
        ef = jnp.concatenate([x[source], x[target]], axis=1)
        h = jax.nn.leaky_relu(layer_norm(ef @ w1 + b1, g1, be1), SLOPE)
        h = jax.nn.leaky_relu(layer_norm(h @ w2 + b2, g2, be2), SLOPE)
        h = h * edge_attr[:, None]
        out = jax.ops.segment_sum(h, target, num_segments=N)
        return out

    def _L1_gnn_ref(x, edge_index, W1_l, b1_l, W1_r, W2_l, b2_l, W2_r):
        import jax, jax.numpy as jnp
        import numpy as np
        N_NODES = 6250
        N_EDGES = 100000
        D_FEAT = 128
        HIDDEN = 128
        OUT = 128

        def _sage_conv(x, src, dst, W_l, b_l, W_r, n_nodes):
            msgs = x[src]
            summed = jax.ops.segment_sum(msgs, dst, num_segments=n_nodes)
            cnt = jax.ops.segment_sum(jnp.ones((src.shape[0],), x.dtype), dst, num_segments=n_nodes)
            aggr = summed / jnp.maximum(cnt, 1.0)[:, None]
            return aggr @ W_l + b_l + x @ W_r
        src, dst = (edge_index[0], edge_index[1])
        n = x.shape[0]
        h = _sage_conv(x, src, dst, W1_l, b1_l, W1_r, n)
        h = jax.nn.relu(h)
        out = _sage_conv(h, src, dst, W2_l, b2_l, W2_r, n)
        return out

    def _L2_gnn_ref(x, edge_index, Wq, Wk, Wl, bl):
        import jax, jax.numpy as jnp
        import numpy as np
        from jax.ops import segment_sum, segment_max
        N_NODES = 6250
        N_EDGES = 200000
        IN_DIM = 128
        OUT_DIM = 128
        N_HEADS = 4
        NEG_SLOPE = 0.2

        def _leaky(v):
            return jnp.where(v >= 0, v, NEG_SLOPE * v)
        num_nodes = x.shape[0]
        row, col = (edge_index[0], edge_index[1])
        h_q = x @ Wq.T
        q_agg = segment_sum(h_q[col], row, num_segments=num_nodes)
        k_act = _leaky(x @ Wk.T)
        scores = k_act[row] * q_agg[col]
        mx = segment_max(scores, row, num_segments=num_nodes)[row]
        ex = jnp.exp(scores - mx)
        sm = segment_sum(ex, row, num_segments=num_nodes)[row]
        alpha = ex / (sm + 1e-08)
        alpha_mean = alpha.mean(axis=1)
        h_proj = x @ Wl.T + bl
        weighted = alpha_mean[:, None] * h_proj[col]
        h_prime = segment_sum(weighted, row, num_segments=num_nodes)
        return _leaky(h_prime)

    def _L3_gnn_ref(x, HE, HEW, W, b):
        import jax, jax.numpy as jnp
        import numpy as np
        N_NODES = 6250
        IN_C = 128
        OUT_C = 128
        N_EDGES = 100000
        N = x.shape[0]
        src, dst = (HE[0], HE[1])
        loop = jnp.arange(N, dtype=HE.dtype)
        src_a = jnp.concatenate([src, loop])
        dst_a = jnp.concatenate([dst, loop])
        w_a = jnp.concatenate([HEW, jnp.ones((N,), dtype=HEW.dtype)])
        deg = jax.ops.segment_sum(w_a, dst_a, num_segments=N)
        dinv = jnp.where(deg > 0, jax.lax.rsqrt(deg), 0.0)
        norm = dinv[src_a] * w_a * dinv[dst_a]
        xw = x @ W
        msg = xw[src_a] * norm[:, None]
        out = jax.ops.segment_sum(msg, dst_a, num_segments=N)
        return out + b
    edge_index = jnp.stack([src, dst])
    h = jnp.maximum(_layernorm(x, axis=-1), 0.0)
    x = x + _L0_gnn_ref(h, edge_index, edge_weight, L0_gnn_w1, L0_gnn_b1, L0_gnn_g1, L0_gnn_be1, L0_gnn_w2, L0_gnn_b2, L0_gnn_g2, L0_gnn_be2)
    h = jnp.maximum(_layernorm(x, axis=-1), 0.0)
    x = x + _L1_gnn_ref(h, edge_index, L1_gnn_W1_l, L1_gnn_b1_l, L1_gnn_W1_r, L1_gnn_W2_l, L1_gnn_b2_l, L1_gnn_W2_r)
    h = jnp.maximum(_layernorm(x, axis=-1), 0.0)
    x = x + _L2_gnn_ref(h, edge_index, L2_gnn_Wq, L2_gnn_Wk, L2_gnn_Wl, L2_gnn_bl)
    h = jnp.maximum(_layernorm(x, axis=-1), 0.0)
    x = x + _L3_gnn_ref(h, edge_index, edge_weight, L3_gnn_W, L3_gnn_b)
    return x

_drawn_inputs = setup_inputs


def setup_inputs(seed=0):
    import zlib

    import numpy as np

    out = dict(_drawn_inputs(seed))
    spreads = {'L0_gnn_g1': (1.0, 0.2),
     'L0_gnn_be1': (0.0, 0.1),
     'L0_gnn_g2': (1.0, 0.2),
     'L0_gnn_be2': (0.0, 0.1),
     'L1_gnn_b1_l': (0.0, 0.8),
     'L1_gnn_b2_l': (0.0, 0.8),
     'L3_gnn_b': (0.0, 0.8)}
    factors = {'L2_gnn_Wq': 8.0, 'L2_gnn_Wk': 8.0, 'L2_gnn_bl': 8.0}
    for name, (base, spread) in spreads.items():
        noise = np.random.default_rng([zlib.crc32(name.encode()), seed]).standard_normal(out[name].shape)
        drawn = base * np.exp(spread * noise) if base else spread * noise
        out[name] = jnp.asarray(drawn.astype(out[name].dtype))
    for name, factor in factors.items():
        out[name] = (out[name] * factor).astype(out[name].dtype)
    return out
```

```python
from contextlib import ExitStack

import numpy as np
import concourse.bass as bass
from concourse import mybir

ALU = mybir.AluOpType
ACT = mybir.ActivationFunctionType
AX_X = mybir.AxisListType.X
F32 = mybir.dt.float32
BF16 = mybir.dt.bfloat16
I32 = mybir.dt.int32

P = 128
C = 128
G = 4
B7 = 7
EPS = 1e-5
IN_WINDOW = "find_windows clamps each tile's window to the groups that exist"
SLOPE = 0.2


class Link:

    def __init__(self, eng, sem, base=0):
        self.eng, self.sem, self.base, self.n = eng, sem, base, 0

    def __call__(self, ins):
        self.n += 1
        ins.then_inc(self.sem, 1)
        self.eng.wait_ge(self.sem, self.base + self.n)


class Sizes:
    def __init__(self, n, e):
        self.N, self.E = n, e
        self.A = -(-n // P)
        self.NP = self.A * P
        self.T = -(-e // (P * 2 * G)) * 2 * G
        self.NG = self.T // G
        self.EP = self.T * P
        self.K = -(-self.T // P)
        assert self.A % B7 == 0


class Mem:

    def __init__(self, nc, ctx, phase):
        self.nc, self.ctx, self.phase, self.sems = nc, ctx, phase, []
        ctx.callback(self.close)

    def sb(self, name, shape, dt=F32):
        return self.ctx.enter_context(self.nc.sbuf_tensor(f"{self.phase}_{name}", shape, dt))

    def psum(self, name, shape, dt=F32):
        return self.ctx.enter_context(self.nc.psum_tensor(f"{self.phase}_{name}", shape, dt))

    def sem(self, name):
        self.sems.append(self.nc.alloc_semaphore(f"{self.phase}_{name}"))
        return self.sems[-1]

    def close(self):
        if self.sems:
            self.nc.clear_and_free_semaphores(self.sems)
            self.nc.all_engine_barrier()


def bcast(ap, n):
    return ap.unsqueeze(2).to_broadcast([ap.shape[0], ap.shape[1], n])


def bcast_mid(ap, n):
    return ap.unsqueeze(1).to_broadcast([ap.shape[0], n, ap.shape[1]])


def node_rows(table, a0, n):
    return table[bass.ds(a0 * P, n * P), :].rearrange("(a p) f -> p a f", p=P)



def make_constants(nc, z, persist):
    k = persist
    z.ident = k.sb("ident", [P, P])
    z.iota = k.sb("iota_row", [P, P])
    z.tile_base = k.sb("tile_base", [P, z.A])
    z.ones = k.sb("ones", [P, P])
    z.zero16 = k.sb("zero16", [P, P], BF16)
    z.zero_wide = k.sb("zero_wide", [P, 512], BF16)
    z.eps = k.sb("eps_col", [P, 1])
    with ExitStack() as ctx:
        m = Mem(nc, ctx, "consts")
        ones_set = m.sem("ones_set")
        with nc.Block() as block:
            @block.gpsimd
            def _(pool):
                pool.memset(z.ones[:], 1.0).then_inc(ones_set, 1)
                pool.memset(z.zero16[:], 0.0)
                pool.memset(z.zero_wide[:], 0.0)
                pool.memset(z.eps[:], EPS)
                pool.iota(z.iota[:], [[1, P]], base=0, channel_multiplier=0, allow_small_or_imprecise_dtypes=True)
                pool.iota(z.tile_base[:], [[-P, z.A]], base=0, channel_multiplier=0,
                          allow_small_or_imprecise_dtypes=True)
                pool.wait_ge(ones_set, 1)
                pool.affine_select(out=z.ident[:], in_=z.ones[:], compare_op=ALU.is_equal, fill=0.0, base=0,
                                   pattern=[[-1, P]], channel_multiplier=1)



def load_edge_lists(nc, z, persist, src, dst, weight):
    T, K, E = z.T, z.K, z.E
    z.srcF = persist.sb("srcF", [P, T])
    z.dstF = persist.sb("dstF", [P, T])
    z.srcI = persist.sb("srcI", [P, T], I32)
    z.dstI = persist.sb("dstI", [P, T], I32)
    z.one_w = persist.sb("one_w", [P, T, 2])
    full = E // P
    tail = E - full * P
    fk = full // P
    fr = full - fk * P
    assert fk == K - 1 and tail > 0
    with ExitStack() as ctx:
        m = Mem(nc, ctx, "lists")
        rows_i = [m.sb(f"rows_i{i}", [P, K, P], I32) for i in range(2)]
        rows_w = m.sb("rows_w", [P, K, P])
        rows_f = [m.sb(f"rows_f{i}", [P, K, P]) for i in range(2)] + [rows_w]
        turned = [m.psum(f"turned{i}", [P, 4 * 512]) for i in range(2)]
        pads_set, rows_in = m.sem("pads_set"), m.sem("rows_in")
        rows_cast, rows_turned, lists_out = m.sem("rows_cast"), m.sem("rows_turned"), m.sem("lists_out")
        with nc.Block() as block:
            @block.gpsimd
            def _(pool):
                for r in rows_i:
                    pool.memset(r[:, K - 1, :], z.NP - 1).then_inc(pads_set, 1)
                pool.memset(rows_w[:, K - 1, :], 0.0).then_inc(pads_set, 1)
                pool.memset(z.one_w[:, :, 0], 1.0)

            @block.sync
            def _(sp):
                sp.wait_ge(pads_set, 3)
                for rows, flat in ((rows_i[0], src), (rows_i[1], dst), (rows_w, weight)):
                    sp.dma_start(rows[:, 0:fk, :], flat[0:fk * P * P].rearrange("(k r c) -> r k c", r=P, c=P)
                                 ).then_inc(rows_in, 16)
                    sp.dma_start(rows[0:fr, fk, :], flat[fk * P * P:full * P].rearrange("(r c) -> r c", c=P)
                                 ).then_inc(rows_in, 16)
                    sp.dma_start(rows[fr:fr + 1, fk, 0:tail], flat[full * P:E].rearrange("(r c) -> r c", r=1)
                                 ).then_inc(rows_in, 16)

            @block.vector
            def _(dve):
                dve.wait_ge(rows_in, 9 * 16)
                for i in range(2):
                    dve.tensor_copy(rows_f[i][:], rows_i[i][:]).then_inc(rows_cast, 1)
                outs = (z.srcF[:], z.dstF[:], z.one_w[:, :, 1])
                for i in range(3):
                    dve.wait_ge(rows_turned, i + 1)
                    for b in range(0, T, 512):
                        n = min(512, T - b)
                        ins = dve.tensor_copy(outs[i][:, b:b + n], turned[i % 2][:, b:b + n])
                    ins.then_inc(lists_out, 1)
                dve.wait_ge(lists_out, 3)
                dve.tensor_copy(z.srcI[:], z.srcF[:])
                dve.tensor_copy(z.dstI[:], z.dstF[:])

            @block.tensor
            def _(pe):
                pe.wait_ge(rows_cast, 2)
                for i in range(3):
                    if i == 2:
                        pe.wait_ge(lists_out, 1)
                    for q in range(K):
                        n = min(P, T - q * P)
                        ins = pe.transpose(turned[i % 2][:, q * P:q * P + n], rows_f[i][0:n, q, :],
                                           z.ident[0:n, 0:n])
                    ins.then_inc(rows_turned, 1)



def find_windows(nc, z, persist, keyF, name, scratch):
    A, NG, T = z.A, z.NG, z.T
    table = persist.sb(f"{name}_windows", [1, A * 3], I32)
    QG = 4
    QC = QG * G
    steps = NG // QG
    assert NG % QG == 0
    with ExitStack() as ctx:
        m = Mem(nc, ctx, f"{name}_win")
        key_i = m.sb("key_i", [P, T], I32)
        tile_i = m.sb("tile_i", [P, T], I32)
        tile_f = m.sb("tile_f", [P, T])
        tiles_row = m.sb("tiles_row", [P, A])
        onehot = [m.sb(f"tile_onehot{i}", [P, QC, A], BF16) for i in range(2)]
        one16 = m.sb("one16", [P, 1], BF16)
        up = m.sb("group_up", [A, NG])
        down = m.sb("group_down", [A, NG])
        seen = m.sb("seen", [A, NG])
        prod = m.sb("window_prod", [A, NG])
        ends = m.sb("window_ends", [A, 4])
        row = m.sb("window_row", [1, A, 2])
        wrk = m.sb("window_wrk", [1, 4, A])
        one_row = m.sb("one_row", [1, A])
        table_f = m.sb("table_f", [1, A, 3])
        count = m.psum("window_count", [A, NG])
        consts, onehot_ready, onehot_used = m.sem("w_consts"), m.sem("w_onehot"), m.sem("w_used")
        link_s, cols_ready, cols_out, row_in = m.sem("w_link"), m.sem("w_cols"), m.sem("w_cols_out"), m.sem("w_row")
        half = steps // 2
        odd = steps % 2
        with nc.Block() as block:
            @block.gpsimd
            def _(pool):
                pool.memset(one16[:], 1.0).then_inc(consts, 1)
                pool.memset(one_row[:], 1.0).then_inc(consts, 1)
                pool.iota(tiles_row[:], [[1, A]], base=0, channel_multiplier=0,
                          allow_small_or_imprecise_dtypes=True).then_inc(consts, 1)
                pool.iota(up[:], [[1, NG]], base=1, channel_multiplier=0,
                          allow_small_or_imprecise_dtypes=True).then_inc(consts, 1)
                pool.iota(down[:], [[-1, NG]], base=NG, channel_multiplier=0,
                          allow_small_or_imprecise_dtypes=True).then_inc(consts, 1)

            @block.vector
            def _(dve):
                link = Link(dve, link_s)
                link(dve.tensor_copy(key_i[:], keyF[:]))
                link(dve.tensor_scalar(tile_i[:], key_i[:], 7, None, ALU.arith_shift_right))
                link(dve.tensor_copy(tile_f[:], tile_i[:]))
                dve.wait_ge(consts, 5)

                def one_hots(step, slot):
                    dve.tensor_tensor(onehot[slot][:], bcast(tile_f[:, bass.ds(step * QC, QC)], A),
                                      bcast_mid(tiles_row[:], QC), ALU.is_equal).then_inc(onehot_ready, 1)

                one_hots(0, 0)
                one_hots(1, 1)
                with dve.Fori(1, half) as i:
                    dve.wait_ge(onehot_used, 2 * i - 1)
                    one_hots(2 * i, 0)
                    dve.wait_ge(onehot_used, 2 * i)
                    one_hots(2 * i + 1, 1)
                if odd:
                    dve.wait_ge(onehot_used, steps - 2)
                    one_hots(steps - 1, 0)
                dve.wait_ge(onehot_used, steps)
                link(dve.tensor_scalar(seen[:], count[:], 1.0, None, ALU.min))
                link(dve.tensor_tensor(prod[:], seen[:], up[:], ALU.mult))
                link(dve.tensor_reduce(ends[:, 1:2], prod[:], AX_X, ALU.max))
                link(dve.tensor_tensor(prod[:], seen[:], down[:], ALU.mult))
                link(dve.tensor_reduce(ends[:, 2:3], prod[:], AX_X, ALU.max))
                link(dve.tensor_scalar(ends[:, 3:4], ends[:, 2:3], -1.0, float(NG), ALU.mult, ALU.add))
                link(dve.tensor_scalar(ends[:, 0:1], ends[:, 3:4], float(NG - 1), None, ALU.min))
                dve.tensor_scalar(ends[:, 2:3], ends[:, 0:1], 1.0, None, ALU.add).then_inc(cols_ready, 1)
                dve.wait_ge(row_in, 16)
                link(dve.tensor_scalar(wrk[:, 0, :], row[:, :, 0], 1.0, None, ALU.add))
                link(dve.tensor_tensor(wrk[:, 1, :], wrk[:, 0, :], row[:, :, 1], ALU.max))
                link(dve.tensor_tensor(wrk[:, 2, :], wrk[:, 1, :], row[:, :, 0], ALU.subtract))
                link(dve.tensor_tensor_scan(wrk[:, 3, :], one_row[:], wrk[:, 2, :], 0.0, ALU.mult, ALU.add))
                link(dve.tensor_tensor(table_f[:, :, 0], wrk[:, 3, :], wrk[:, 2, :], ALU.subtract))
                link(dve.tensor_copy(table_f[:, :, 1], wrk[:, 3, :]))
                link(dve.tensor_tensor(table_f[:, :, 2], wrk[:, 1, :], wrk[:, 3, :], ALU.subtract))
                dve.tensor_copy(table[:], table_f[:].rearrange("o a k -> o (a k)"))

            @block.tensor
            def _(pe):
                pe.wait_ge(consts, 5)

                def counts(step, slot):
                    pe.wait_ge(onehot_ready, step + 1)
                    for q in range(QG):
                        for j in range(G):
                            ins = pe.matmul(count[:, bass.ds(step * QG + q, 1)], onehot[slot][:, q * G + j, :],
                                            one16[:], start=j == 0, stop=j == G - 1)
                    ins.then_inc(onehot_used, 1)

                with pe.Fori(0, half) as i:
                    counts(2 * i, 0)
                    counts(2 * i + 1, 1)
                if odd:
                    counts(steps - 1, 0)

            @block.sync
            def _(sp):
                sp.wait_ge(cols_ready, 1)
                sp.dma_start(scratch, ends[:, 0:2]).then_inc(cols_out, 16)
                sp.wait_ge(cols_out, 16)
                sp.dma_start(row[:], scratch.rearrange("(o a) k -> o a k", o=1)).then_inc(row_in, 16)
    return table



def segment_sum(nc, z, name, windows, keyF, out, gather=None, rows=None, scale=None, extras=None, extras_out=None):
    A, NG = z.A, z.NG
    maxv = A * NG
    with ExitStack() as ctx:
        m = Mem(nc, ctx, name)
        data = m.sb("rows", [P, G, C])
        scaled = m.sb("rows_scaled", [P, G, C]) if scale is not None else data
        onehot = m.sb("onehot", [P, G, P])
        acc = m.psum("acc", [P, P])
        acc_x = m.psum("acc_x", [P, 2])
        landed = [m.sem(f"landed{j}") for j in range(G)]
        scaled_ready = m.sem("scaled_ready")
        products_done = m.sem("products_done")
        onehot_ready = m.sem("onehot_ready")
        stage = m.sb("index_stage", [P, G], I32)
        staged = m.sem("staged")
        waited = m.sem("waited")
        tile_summed, tile_stored = m.sem("tile_summed"), m.sem("tile_stored")

        def window(eng, a):
            before = eng.value_load(windows[0:1, bass.ds(a * 3, 1)], min_val=0, max_val=maxv)
            after = eng.value_load(windows[0:1, bass.ds(a * 3 + 1, 1)], min_val=1, max_val=maxv)
            shift = eng.value_load(windows[0:1, bass.ds(a * 3 + 2, 1)], min_val=-maxv, max_val=NG)
            return before, after, shift

        with nc.Block() as block:
            def loader(eng):
                with eng.Fori(0, A) as a:
                    before, after, shift = window(eng, a)
                    with eng.Fori(before, after) as v:
                        g = nc.s_assert_within(v + shift, 0, NG - 1, skip_runtime_bounds_check_because=IN_WINDOW)
                        for j in range(G):
                            if gather is not None:
                                eng.wait_ge(staged, v * G + (j + 1))
                                eng.sem_inc(waited, 1)
                                eng.indirect_dma_start(
                                    data[:, j, :], None, gather[0],
                                    bass.IndirectOffsetOnAxis(ap=stage[:, j:j + 1], axis=0),
                                ).then_inc(landed[j], 16)
                            else:
                                eng.wait_ge(scaled_ready if scale is not None else products_done,
                                            v * G + (j + 1))
                                eng.dma_start(data[:, j, :], rows[bass.ds((g * G + j) * P, P), :]
                                              ).then_inc(landed[j], 16)

            if gather is not None:
                @block.gpsimd
                def _(pool):
                    loader(pool)
            else:
                @block.sync
                def _(sp):
                    loader(sp)

            @block.vector
            def _(dve):
                dve.sem_inc(tile_stored, 1)
                with dve.Fori(0, A) as a:
                    before, after, shift = window(dve, a)
                    with dve.Fori(before, after) as v:
                        g = nc.s_assert_within(v + shift, 0, NG - 1, skip_runtime_bounds_check_because=IN_WINDOW)
                        for j in range(G):
                            dve.wait_ge(products_done, v * G + (j + 1))
                            if gather is not None:
                                dve.tensor_copy(stage[:, j:j + 1], gather[1][:, bass.ds(g * G + j, 1)]
                                                ).then_inc(staged, 1)
                            dve.tensor_scalar(onehot[:, j, :], z.iota[:], keyF[:, bass.ds(g * G + j, 1)],
                                              z.tile_base[:, bass.ds(a, 1)], ALU.subtract, ALU.is_equal
                                              ).then_inc(onehot_ready, 1)
                    dve.wait_ge(tile_summed, a + 1)
                    ins = dve.tensor_copy(out[:, bass.ds(a, 1), :], acc[:].unsqueeze(1))
                    if extras is not None:
                        ins = dve.tensor_copy(extras_out[:, bass.ds(a, 1), :], acc_x[:].unsqueeze(1))
                    ins.then_inc(tile_stored, 1)

            @block.tensor
            def _(pe):
                pe.sem_inc(products_done, G)
                with pe.Fori(0, A) as a:
                    before, after, shift = window(pe, a)
                    pe.wait_ge(tile_stored, a + 1)
                    pe.matmul(acc[:], z.zero16[:, 0:P], z.zero16[:, 0:P], start=True, stop=False)
                    if extras is not None:
                        pe.matmul(acc_x[:], z.zero16[:, 0:P], z.zero16[:, 0:2], start=True, stop=False)
                    with pe.Fori(before, after) as v:
                        g = nc.s_assert_within(v + shift, 0, NG - 1, skip_runtime_bounds_check_because=IN_WINDOW)
                        for j in range(G):
                            if scale is not None:
                                pe.wait_ge(scaled_ready, v * G + (G + j + 1))
                            else:
                                pe.wait_ge(landed[j], v * 16 + 16)
                            pe.wait_ge(onehot_ready, v * G + (j + 1))
                            if extras is not None:
                                pe.matmul(acc_x[:], onehot[:, j, :], extras[:, bass.ds(g * G + j, 1), :],
                                          start=False, stop=False)
                            pe.matmul(acc[:], onehot[:, j, :], scaled[:, j, :], start=False, stop=False
                                      ).then_inc(products_done, 1)
                    if extras is not None:
                        pe.matmul(acc_x[:], z.zero16[:, 0:P], z.zero16[:, 0:2], start=False, stop=True)
                    pe.matmul(acc[:], z.zero16[:, 0:P], z.zero16[:, 0:P], start=False, stop=True
                              ).then_inc(tile_summed, 1)

            if scale is not None:
                @block.scalar
                def _(act):
                    act.sem_inc(scaled_ready, G)
                    with act.Fori(0, A) as a:
                        before, after, shift = window(act, a)
                        with act.Fori(before, after) as v:
                            g = nc.s_assert_within(v + shift, 0, NG - 1, skip_runtime_bounds_check_because=IN_WINDOW)
                            for j in range(G):
                                act.wait_ge(landed[j], v * 16 + 16)
                                act.wait_ge(products_done, v * G + (j + 1))
                                act.activation(scaled[:, j, :], data[:, j, :], ACT.Copy,
                                               scale=scale[:, bass.ds(g * G + j, 1)]).then_inc(scaled_ready, 1)



def norm_relu(dve, link, act_var, act_std, seq, x, out, b):
    dve.sem_inc(b.waited, 1)
    link(dve.tensor_reduce(b.mean[:], x, AX_X, ALU.add))
    link(dve.tensor_scalar(b.mean[:], b.mean[:], -1.0 / C, None, ALU.mult))
    link(dve.tensor_tensor(b.cent[:], x, bcast(b.mean[:], C), ALU.add))
    link(dve.tensor_tensor(b.sq[:], b.cent[:], b.cent[:], ALU.mult))
    dve.tensor_reduce(b.var[:], b.sq[:], AX_X, ALU.add).then_inc(act_var, 1)
    dve.wait_ge(act_std, seq)
    link(dve.reciprocal(b.rstd[:], b.std[:]))
    link(dve.tensor_tensor(b.sq[:], b.cent[:], bcast(b.rstd[:], C), ALU.mult))
    link(dve.tensor_scalar(out, b.sq[:], 0.0, None, ALU.max))


class NormBuffers:
    LINKS = 7

    def __init__(self, m):
        self.waited = m.sem("waited")
        self.mean = m.sb("n_mean", [P, B7])
        self.cent = m.sb("n_cent", [P, B7, C])
        self.sq = m.sb("n_sq", [P, B7, C])
        self.var = m.sb("n_var", [P, B7])
        self.std = m.sb("n_std", [P, B7])
        self.rstd = m.sb("n_rstd", [P, B7])


def act_root(act, z, b, act_var, act_std, seq):
    act.wait_ge(act_var, seq)
    act.activation(b.std[:], b.var[:], ACT.Sqrt, bias=z.eps[:], scale=1.0 / C).then_inc(act_std, 1)


def entry(nc, z, x, tabA, tabB, w1, b1):
    A = z.A
    steps = A // B7
    with ExitStack() as ctx:
        m = Mem(nc, ctx, "entry")
        b = NormBuffers(m)
        h = m.sb("h", [P, B7, C])
        hT = m.sb("hT", [P, B7, P])
        w = m.sb("w_ab", [P, 2, C])
        wc = m.sb("w_ab_centred", [P, 2, C])
        wm = m.sb("w_ab_mean", [P, 2])
        bias = m.sb("bias_ab", [1, 2, C])
        brow = m.sb("b1_row", [1, C])
        bm = m.sb("b1_mean", [1, 1])
        ab = m.sb("ab", [P, A, 2 * C])
        psT = m.psum("psT", [P, 8, P])
        psM = m.psum("psM", [P, 8, 2 * C])
        x_in, x_pad, w_in, links = m.sem("x_in"), m.sem("x_pad"), m.sem("w_in"), m.sem("links")
        var_ready, std_ready, h_ready = m.sem("var_ready"), m.sem("std_ready"), m.sem("h_ready")
        t_ready, hT_ready, m_ready, w_ready = m.sem("t_ready"), m.sem("hT_ready"), m.sem("m_ready"), m.sem("w_ready")
        ab_ready, ab_out = m.sem("ab_ready"), m.sem("ab_out")
        fullt = z.N // P
        rest = z.N - fullt * P
        L = NormBuffers.LINKS + 1
        with nc.Block() as block:
            @block.gpsimd
            def _(pool):
                pool.memset(z.X[:, A - 1, :], 0.0).then_inc(x_pad, 1)

            @block.sync
            def _(sp):
                sp.dma_start(z.X[:, 0:fullt, :], x[0:fullt * P, :].rearrange("(a p) f -> p a f", p=P)
                             ).then_inc(x_in, 16)
                sp.dma_start(w[:], w1.rearrange("(h k) f -> k h f", h=2)).then_inc(w_in, 16)
                sp.dma_start(brow[:], b1.rearrange("(o f) -> o f", o=1)).then_inc(w_in, 16)
                sp.wait_ge(x_pad, 1)
                sp.dma_start(z.X[0:rest, fullt, :], x[fullt * P:z.N, :]).then_inc(x_in, 16)
                sp.wait_ge(ab_ready, steps)
                sp.dma_start(node_rows(tabA, 0, A), ab[:, :, 0:C]).then_inc(ab_out, 16)
                sp.dma_start(node_rows(tabB, 0, A), ab[:, :, C:2 * C]).then_inc(ab_out, 16)
                sp.wait_ge(ab_out, 32)

            @block.vector
            def _(dve):
                pre = Link(dve, links)
                dve.wait_ge(w_in, 32)
                pre(dve.tensor_reduce(wm[:], w[:], AX_X, ALU.add))
                pre(dve.tensor_scalar(wm[:], wm[:], -1.0 / C, None, ALU.mult))
                pre(dve.tensor_tensor(wc[:], w[:], bcast(wm[:], C), ALU.add))
                pre(dve.memset(bias[:], 0.0))
                pre(dve.tensor_reduce(bm[:], brow[:], AX_X, ALU.add))
                pre(dve.tensor_scalar(bm[:], bm[:], -1.0 / C, None, ALU.mult))
                dve.tensor_scalar(bias[:, 1, :], brow[:], bm[:, 0:1], None, ALU.add).then_inc(w_ready, 1)
                dve.wait_ge(x_in, 32)
                with dve.Fori(0, steps) as i:
                    link = Link(dve, links, pre.n + i * L)
                    norm_relu(dve, link, var_ready, std_ready, i + 1, z.X[:, bass.ds(i * B7, B7), :], h[:], b)
                    dve.sem_inc(h_ready, 1)
                    dve.wait_ge(m_ready, i + 1)
                    link(dve.tensor_copy(ab[:, bass.ds(i * B7, B7), :], psM[:, 0:B7, :]))
                    dve.sem_inc(ab_ready, 1)

            @block.scalar
            def _(act):
                with act.Fori(0, steps) as i:
                    act_root(act, z, b, var_ready, std_ready, i + 1)
                    act.wait_ge(t_ready, i + 1)
                    act.activation(hT[:], psT[:, 0:B7, :], ACT.Copy).then_inc(hT_ready, 1)

            @block.tensor
            def _(pe):
                pe.wait_ge(w_ready, 1)
                with pe.Fori(0, steps) as i:
                    pe.wait_ge(h_ready, i + 1)
                    for j in range(B7):
                        ins = pe.transpose(psT[:, j, :], h[:, j, :], z.ident[:])
                    ins.then_inc(t_ready, 1)
                    pe.wait_ge(hT_ready, i + 1)
                    for j in range(B7):
                        pe.matmul(psM[:, j, :], z.ones[0:1, :], bias[:].rearrange("o h f -> o (h f)"),
                                  start=True, stop=False)
                        ins = pe.matmul(psM[:, j, :], hT[:, j, :], wc[:].rearrange("k h f -> k (h f)"),
                                        start=False, stop=True)
                    ins.then_inc(m_ready, 1)


def edge_mlp(nc, z, tabA, tabB, msg, w2, b2, g1, be1, g2, be2):
    NG = z.NG
    with ExitStack() as ctx:
        m = Mem(nc, ctx, "mlp")
        ga = m.sb("ga", [P, 2, G, C])
        gb = m.sb("gb", [P, 2, G, C])
        stage = m.sb("index_stage", [P, 2, 2, G], I32)
        staged, waited = m.sem("staged"), m.sem("waited")
        u = m.sb("u", [P, 2, G, C])
        y = m.sb("y", [P, 2, G, C])
        vT = m.sb("vT", [P, 2, G, P])
        zT = m.sb("zT", [P, 2, G, P])
        y2 = m.sb("y2", [P, 2, G, C])
        y3 = m.sb("y3", [P, 2, G, C])
        out = m.sb("msg_rows", [P, 2, G, C])
        junk = m.sb("squares", [P, 2, 2, G, C])
        var = m.sb("var", [P, 2, 2, G])
        std = m.sb("std", [P, 2, 2, G])
        rstd = m.sb("rstd", [P, 2, 2, G])
        cols = m.sb("cols", [P, 2])
        rowsb = m.sb("rowsb", [P, 2, C])
        w = m.sb("w2", [P, C])
        wc = m.sb("w2_centred", [P, C])
        wm = m.sb("w2_mean", [P, 1])
        brow = m.sb("b2_row", [1, C])
        bias = m.sb("b2_centred", [1, C])
        bm = m.sb("b2_mean", [1, 1])
        psT = m.psum("psT", [P, 2, G * P])
        psH = m.psum("psH", [P, 2, G, P])
        gathered = [m.sem(f"gathered{q}") for q in range(2)]
        w_in, w_ready, links = m.sem("w_in"), m.sem("w_ready"), m.sem("links")
        u_ready, var1, std1, r1, y_ready = (m.sem(s) for s in ("u_ready", "var1_ready", "std1_ready", "r1_ready", "y_ready"))
        t_ready, z_ready, h_ready = m.sem("t_ready"), m.sem("z_ready"), m.sem("h_ready")
        v_ready = m.sem("v_ready")
        var2, std2, r2, y2_ready, y3_ready = (m.sem(s) for s in ("var2_ready", "std2_ready", "r2_ready", "y2_ready", "y3_ready"))
        out_ready = m.sem("out_ready")
        stored = [m.sem(f"stored{q}") for q in range(2)]

        def skewed(eng, first, second):
            first(0, 0)
            first(1, 1)
            second(0, 0)
            with eng.Fori(1, NG // 2) as i:
                first(2 * i, 0)
                second(2 * i - 1, 1)
                first(2 * i + 1, 1)
                second(2 * i, 0)
            second(NG - 1, 1)

        with nc.Block() as block:
            @block.gpsimd
            def _(pool):
                def gathers(g, q):
                    if not (isinstance(g, int) and g < 2):
                        pool.wait_ge(u_ready, g - 1)
                        pool.sem_inc(waited, 1)
                    pool.tensor_copy(stage[:, q, 0, :], z.srcI[:, bass.ds(g * G, G)]).then_inc(staged, 1)
                    pool.tensor_copy(stage[:, q, 1, :], z.dstI[:, bass.ds(g * G, G)]).then_inc(staged, 1)
                    pool.wait_ge(staged, g * 2 + 2)
                    pool.sem_inc(waited, 1)
                    for j in range(G):
                        for side, table, rows in ((0, tabA, ga), (1, tabB, gb)):
                            pool.indirect_dma_start(
                                rows[:, q, j, :], None, table,
                                bass.IndirectOffsetOnAxis(ap=stage[:, q, side, j:j + 1], axis=0),
                            ).then_inc(gathered[q], 16)
                gathers(0, 0)
                gathers(1, 1)
                with pool.Fori(1, NG // 2) as i:
                    gathers(2 * i, 0)
                    gathers(2 * i + 1, 1)

            @block.sync
            def _(sp):
                sp.dma_start(w[:], w2).then_inc(w_in, 16)
                sp.dma_start(brow[:], b2.rearrange("(o f) -> o f", o=1)).then_inc(w_in, 16)
                sp.dma_start(cols[:, 0:1], g1.rearrange("(f o) -> f o", o=1)).then_inc(w_in, 16)
                sp.dma_start(cols[:, 1:2], be1.rearrange("(f o) -> f o", o=1)).then_inc(w_in, 16)
                sp.dma_start(rowsb[:, 0, :], g2.partition_broadcast(P)).then_inc(w_in, 16)
                sp.dma_start(rowsb[:, 1, :], be2.partition_broadcast(P)).then_inc(w_in, 16)

                def store(g, q):
                    sp.wait_ge(out_ready, g + 1)
                    sp.dma_start(msg[bass.ds(g * G * P, G * P), :].rearrange("(j p) f -> p j f", p=P),
                                 out[:, q, :, :]).then_inc(stored[q], 16)
                with sp.Fori(0, NG // 2) as i:
                    store(2 * i, 0)
                    store(2 * i + 1, 1)
                sp.wait_ge(stored[0], 16 * (NG // 2))
                sp.wait_ge(stored[1], 16 * (NG // 2))

            @block.vector
            def _(dve):
                pre = Link(dve, links)
                dve.wait_ge(w_in, 6 * 16)
                pre(dve.tensor_reduce(wm[:], w[:], AX_X, ALU.add))
                pre(dve.tensor_scalar(wm[:], wm[:], -1.0 / C, None, ALU.mult))
                dve.tensor_scalar(wc[:], w[:], wm[:, 0:1], None, ALU.add).then_inc(w_ready, 1)
                pre(dve.tensor_reduce(bm[:], brow[:], AX_X, ALU.add))
                pre(dve.tensor_scalar(bm[:], bm[:], -1.0 / C, None, ALU.mult))
                dve.tensor_scalar(bias[:], brow[:], bm[:, 0:1], None, ALU.add).then_inc(w_ready, 1)

                def layer1(g, q):
                    first = isinstance(g, int) and g < 2
                    dve.wait_ge(gathered[q], (g // 2 + 1) * 2 * G * 16 if isinstance(g, int) else (g + (2 - q)) * G * 16)
                    if not first:
                        dve.wait_ge(t_ready, g - 1)
                    dve.tensor_tensor(u[:, q, :, :], ga[:, q, :, :], gb[:, q, :, :], ALU.add).then_inc(u_ready, 1)
                    dve.wait_ge(std1, g + 1)
                    dve.reciprocal(rstd[:, q, 0, :], std[:, q, 0, :]).then_inc(r1, 1)
                    dve.wait_ge(r1, g + 1)
                    for j in range(G):
                        ins = dve.tensor_scalar(y[:, q, j, :], u[:, q, j, :], rstd[:, q, 0, j:j + 1], None, ALU.mult)
                    ins.then_inc(y_ready, 1)

                def layer2(g, q):
                    dve.wait_ge(v_ready, g + 1)
                    if not (isinstance(g, int) and g < 2):
                        dve.wait_ge(h_ready, g - 1)
                    dve.scalar_tensor_tensor(out=zT[:, q, :, :], in0=vT[:, q, :, :], scalar=SLOPE, in1=vT[:, q, :, :],
                                             op0=ALU.mult, op1=ALU.max).then_inc(z_ready, 1)
                    dve.wait_ge(std2, g + 1)
                    dve.reciprocal(rstd[:, q, 1, :], std[:, q, 1, :]).then_inc(r2, 1)
                    dve.wait_ge(r2, g + 1)
                    for j in range(G):
                        ins = dve.scalar_tensor_tensor(out=y2[:, q, j, :], in0=psH[:, q, j, :],
                                                       scalar=rstd[:, q, 1, j:j + 1], in1=rowsb[:, 0, :],
                                                       op0=ALU.mult, op1=ALU.mult)
                    ins.then_inc(y2_ready, 1)
                    dve.wait_ge(y2_ready, g + 1)
                    dve.tensor_tensor(y3[:, q, :, :], y2[:, q, :, :], bcast_mid(rowsb[:, 1, :], G), ALU.add
                                      ).then_inc(y3_ready, 1)
                    dve.wait_ge(y3_ready, g + 1)
                    if not (isinstance(g, int) and g < 2):
                        dve.wait_ge(stored[q], (g - q) * 8)
                    dve.scalar_tensor_tensor(out=out[:, q, :, :], in0=y3[:, q, :, :], scalar=SLOPE,
                                             in1=y3[:, q, :, :], op0=ALU.mult, op1=ALU.max).then_inc(out_ready, 1)
                skewed(dve, layer1, layer2)

            @block.scalar
            def _(act):
                def layer1(g, q):
                    act.wait_ge(u_ready, g + 1)
                    for j in range(G):
                        ins = act.activation(junk[:, q, 0, j, :], u[:, q, j, :], ACT.Square, accum_out=var[:, q, 0, j:j + 1])
                    ins.then_inc(var1, 1)
                    act.wait_ge(var1, g + 1)
                    if not (isinstance(g, int) and g < 2):
                        act.wait_ge(r1, g - 1)
                    act.activation(std[:, q, 0, :], var[:, q, 0, :], ACT.Sqrt, bias=z.eps[:], scale=1.0 / C
                                   ).then_inc(std1, 1)
                    act.wait_ge(t_ready, g + 1)
                    if not (isinstance(g, int) and g < 2):
                        act.wait_ge(z_ready, g - 1)
                    act.activation(vT[:, q, :, :], psT[:, q, :].rearrange("p (j e) -> p j e", j=G), ACT.Identity,
                                   bias=cols[:, 1:2], scale=cols[:, 0:1]).then_inc(v_ready, 1)

                def layer2(g, q):
                    act.wait_ge(h_ready, g + 1)
                    for j in range(G):
                        ins = act.activation(junk[:, q, 1, j, :], psH[:, q, j, :], ACT.Square, accum_out=var[:, q, 1, j:j + 1])
                    ins.then_inc(var2, 1)
                    act.wait_ge(var2, g + 1)
                    act.activation(std[:, q, 1, :], var[:, q, 1, :], ACT.Sqrt, bias=z.eps[:], scale=1.0 / C
                                   ).then_inc(std2, 1)
                act.wait_ge(w_in, 6 * 16)
                skewed(act, layer1, layer2)

            @block.tensor
            def _(pe):
                def layer1(g, q):
                    pe.wait_ge(y_ready, g + 1)
                    if not (isinstance(g, int) and g < 2):
                        pe.wait_ge(v_ready, g - 1)
                    for j in range(G):
                        ins = pe.transpose(psT[:, q, j * P:(j + 1) * P], y[:, q, j, :], z.ident[:])
                    ins.then_inc(t_ready, 1)

                def layer2(g, q):
                    pe.wait_ge(z_ready, g + 1)
                    if not (isinstance(g, int) and g < 2):
                        pe.wait_ge(y2_ready, g - 1)
                    for j in range(G):
                        pe.matmul(psH[:, q, j, :], z.ones[0:1, :], bias[:], start=True, stop=False)
                        ins = pe.matmul(psH[:, q, j, :], zT[:, q, j, :], wc[:], start=False, stop=True)
                    ins.then_inc(h_ready, 1)
                pe.wait_ge(w_ready, 2)
                skewed(pe, layer1, layer2)



def after_mlp(nc, z, tabH):
    A = z.A
    steps = A // B7
    with ExitStack() as ctx:
        m = Mem(nc, ctx, "after_mlp")
        b = NormBuffers(m)
        links, var_ready, std_ready = m.sem("links"), m.sem("var_ready"), m.sem("std_ready")
        h_ready, h_out = m.sem("h_ready"), m.sem("h_out")
        L = NormBuffers.LINKS + 1
        with nc.Block() as block:
            @block.sync
            def _(sp):
                sp.wait_ge(h_ready, steps)
                sp.dma_start(node_rows(tabH, 0, A), z.H[:]).then_inc(h_out, 16)
                sp.wait_ge(h_out, 16)

            @block.vector
            def _(dve):
                with dve.Fori(0, steps) as i:
                    link = Link(dve, links, i * L)
                    xs = z.X[:, bass.ds(i * B7, B7), :]
                    link(dve.tensor_tensor(xs, xs, z.SUM[:, bass.ds(i * B7, B7), :], ALU.add))
                    norm_relu(dve, link, var_ready, std_ready, i + 1, xs, z.H[:, bass.ds(i * B7, B7), :], b)
                    dve.sem_inc(h_ready, 1)

            @block.scalar
            def _(act):
                with act.Fori(0, steps) as i:
                    act_root(act, z, b, var_ready, std_ready, i + 1)


def sage_layer(nc, z, name, w_l, b_l, w_r, hidden_table=None, attention=None):
    A = z.A
    steps = A // B7
    D = 4 + 4 + C
    with ExitStack() as ctx:
        m = Mem(nc, ctx, name)
        mean = m.sb("mean", [P, B7, C])
        hs = m.sb("hs", [P, B7, C])
        turned = m.sb("turned", [P, 2 * B7, P])
        wl, wr, brow = m.sb("wl", [P, C]), m.sb("wr", [P, C]), m.sb("brow", [1, C])
        psT = m.psum("psT", [P, 4 * 4, P])
        psM = m.psum("psM", [P, 8, 2 * C])
        w_in, links, raw_set = m.sem("w_in"), m.sem("links"), m.sem("raw_set")
        bias_set = m.sem("bias_set")
        in_ready, t_ready, turned_ready, m_ready = (m.sem(s) for s in ("in_ready", "t_ready", "turned_ready", "m_ready"))
        var_ready, std_ready = m.sem("var_ready"), m.sem("std_ready")
        t2_ready, turned2_ready, m2_ready = m.sem("t2_ready"), m.sem("turned2_ready"), m.sem("m2_ready")
        h3_ready, tabs_ready, tabs_out = m.sem("h3_ready"), m.sem("tabs_ready"), m.sem("tabs_out")
        weights_turned, weights_ready = m.sem("weights_turned"), m.sem("weights_ready")
        last = attention is not None
        if last:
            wq, wk, wo, bo, tabQ, tabK, tabV = attention
            b = NormBuffers(m)
            h3 = m.sb("h3", [P, B7, C])
            raw = m.sb("raw", [P, 2, P])
            wcat = m.sb("wcat", [P, D])
            bcat = m.sb("bcat", [1, D])
            qk = m.sb("qk", [P, A, 8])
            qk0 = m.sb("qk0", [P, B7, 4])
            hv = m.sb("hv", [P, A, C])
            L = 3 + 1 + NormBuffers.LINKS + 4
        else:
            L = 3 + 1
        PRE = 0 if last else 2

        with nc.Block() as block:
            @block.sync
            def _(sp):
                sp.dma_start(wl[:], w_l).then_inc(w_in, 16)
                sp.dma_start(wr[:], w_r).then_inc(w_in, 16)
                sp.dma_start(brow[:], b_l.rearrange("(o f) -> o f", o=1)).then_inc(w_in, 16)
                if last:
                    sp.wait_ge(raw_set, 1)
                    sp.wait_ge(bias_set, 1)
                    sp.dma_start(raw[0:4, 0, :], wq).then_inc(w_in, 16)
                    sp.dma_start(raw[4:8, 0, :], wk).then_inc(w_in, 16)
                    sp.dma_start(raw[:, 1, :], wo).then_inc(w_in, 16)
                    sp.dma_start(bcat[:, 8:D], bo.rearrange("(o f) -> o f", o=1)).then_inc(w_in, 16)
                sp.wait_ge(tabs_ready, steps)
                if last:
                    sp.dma_start(node_rows(tabQ, 0, A), qk[:, :, 0:4]).then_inc(tabs_out, 16)
                    sp.dma_start(node_rows(tabK, 0, A), qk[:, :, 4:8]).then_inc(tabs_out, 16)
                    sp.dma_start(node_rows(tabV, 0, A), hv[:]).then_inc(tabs_out, 16)
                    sp.wait_ge(tabs_out, 48)
                else:
                    sp.dma_start(node_rows(hidden_table, 0, A), z.H[:]).then_inc(tabs_out, 16)
                    sp.wait_ge(tabs_out, 16)

            @block.vector
            def _(dve):
                if last:
                    dve.memset(bcat[:], 0.0).then_inc(bias_set, 1)
                    dve.wait_ge(weights_turned, 1)
                    dve.tensor_copy(wcat[:, 0:8], psT[:, 0, 0:8]).then_inc(weights_ready, 1)
                    dve.tensor_copy(wcat[:, 8:D], psT[:, 1, :]).then_inc(weights_ready, 1)
                else:
                    pre = Link(dve, links)
                    pre(dve.tensor_scalar(z.rcount[:], z.SUMX[:, :, 0], 1.0, None, ALU.max))
                    pre(dve.reciprocal(z.rcount[:], z.rcount[:]))
                with dve.Fori(0, steps) as i:
                    link = Link(dve, links, PRE + i * L)
                    tiles = bass.ds(i * B7, B7)
                    link(dve.tensor_tensor(mean[:], z.SUM[:, tiles, :], bcast(z.rcount[:, tiles], C), ALU.mult))
                    link(dve.tensor_copy(hs[:], z.H[:, tiles, :]))
                    dve.sem_inc(in_ready, 1)
                    dve.wait_ge(m_ready, i + 1)
                    if not last:
                        link(dve.tensor_scalar(z.H[:, tiles, :], psM[:, 0:B7, 0:C], 0.0, None, ALU.max))
                        link(dve.memset(mean[:, 0, 0:1], 0.0))
                        dve.sem_inc(tabs_ready, 1)
                    else:
                        link(dve.tensor_tensor(z.X[:, tiles, :], z.X[:, tiles, :], psM[:, 0:B7, 0:C], ALU.add))
                        norm_relu(dve, link, var_ready, std_ready, i + 1, z.X[:, tiles, :], h3[:], b)
                        dve.sem_inc(h3_ready, 1)
                        dve.wait_ge(m2_ready, i + 1)
                        link(dve.tensor_copy(hv[:, tiles, :], psM[:, 0:B7, 8:D]))
                        link(dve.tensor_copy(qk[:, tiles, 0:4], psM[:, 0:B7, 0:4]))
                        link(dve.tensor_scalar(qk0[:], psM[:, 0:B7, 4:8], SLOPE, None, ALU.mult))
                        link(dve.tensor_tensor(qk[:, tiles, 4:8], psM[:, 0:B7, 4:8], qk0[:], ALU.max))
                        link(dve.memset(mean[:, 0, 0:1], 0.0))
                        dve.sem_inc(tabs_ready, 1)

            @block.scalar
            def _(act):
                with act.Fori(0, steps) as i:
                    act.wait_ge(t_ready, i + 1)
                    act.activation(turned[:], psT[:, 0:2 * B7, :], ACT.Copy).then_inc(turned_ready, 1)
                    if last:
                        act_root(act, z, b, var_ready, std_ready, i + 1)
                        act.wait_ge(t2_ready, i + 1)
                        act.activation(turned[:, 0:B7, :], psT[:, 0:B7, :], ACT.Copy).then_inc(turned2_ready, 1)

            @block.gpsimd
            def _(pool):
                if last:
                    pool.memset(raw[:, 0, :], 0.0).then_inc(raw_set, 1)

            @block.tensor
            def _(pe):
                pe.wait_ge(w_in, (7 if last else 3) * 16)
                if last:
                    pe.transpose(psT[:, 0, :], raw[:, 0, :], z.ident[:])
                    pe.transpose(psT[:, 1, :], raw[:, 1, :], z.ident[:]).then_inc(weights_turned, 1)
                    pe.wait_ge(weights_ready, 2)
                with pe.Fori(0, steps) as i:
                    pe.wait_ge(in_ready, i + 1)
                    for j in range(B7):
                        pe.transpose(psT[:, 2 * j, :], mean[:, j, :], z.ident[:])
                        ins = pe.transpose(psT[:, 2 * j + 1, :], hs[:, j, :], z.ident[:])
                    ins.then_inc(t_ready, 1)
                    pe.wait_ge(turned_ready, i + 1)
                    for j in range(B7):
                        pe.matmul(psM[:, j, 0:C], z.ones[0:1, :], brow[:], start=True, stop=False)
                        pe.matmul(psM[:, j, 0:C], turned[:, 2 * j, :], wl[:], start=False, stop=False)
                        ins = pe.matmul(psM[:, j, 0:C], turned[:, 2 * j + 1, :], wr[:], start=False, stop=True)
                    ins.then_inc(m_ready, 1)
                    if last:
                        pe.wait_ge(h3_ready, i + 1)
                        for j in range(B7):
                            ins = pe.transpose(psT[:, j, :], h3[:, j, :], z.ident[:])
                        ins.then_inc(t2_ready, 1)
                        pe.wait_ge(turned2_ready, i + 1)
                        for j in range(B7):
                            pe.matmul(psM[:, j, 0:D], z.ones[0:1, :], bcat[:], start=True, stop=False)
                            ins = pe.matmul(psM[:, j, 0:D], turned[:, j, :], wcat[:], start=False, stop=True)
                        ins.then_inc(m2_ready, 1)


def after_attention(nc, z, tabX, w):
    A = z.A
    steps = A // B7
    with ExitStack() as ctx:
        m = Mem(nc, ctx, "after_attention")
        b = NormBuffers(m)
        act7 = m.sb("leaky", [P, B7, C])
        h = m.sb("h", [P, B7, C])
        hT = m.sb("hT", [P, B7, P])
        ws = m.sb("w", [P, C])
        degree, above, root = m.sb("degree", [P, A]), m.sb("above", [P, A]), m.sb("root", [P, A])
        psT = m.psum("psT", [P, 8, P])
        psM = m.psum("psM", [P, 8, C])
        names = ("w_in", "links", "degree_ready", "root_ready", "var_ready", "std_ready", "h_ready", "t_ready",
                 "hT_ready", "m_ready", "tab_ready", "tab_out")
        (w_in, links, degree_ready, root_ready, var_ready, std_ready, h_ready, t_ready, hT_ready, m_ready, tab_ready,
         tab_out) = (m.sem(s) for s in names)
        L = 2 + NormBuffers.LINKS + 1
        with nc.Block() as block:
            @block.sync
            def _(sp):
                sp.dma_start(ws[:], w).then_inc(w_in, 16)
                sp.wait_ge(tab_ready, steps)
                sp.dma_start(node_rows(tabX, 0, A), z.H[:]).then_inc(tab_out, 16)
                sp.wait_ge(tab_out, 16)

            @block.vector
            def _(dve):
                pre = Link(dve, links)
                pre(dve.tensor_scalar(degree[:], z.SUMX[:, :, 1], 1.0, None, ALU.add))
                pre(dve.tensor_scalar(above[:], degree[:], 0.0, None, ALU.is_gt))
                dve.tensor_scalar(degree[:], degree[:], 1e-30, None, ALU.max).then_inc(degree_ready, 1)
                dve.wait_ge(root_ready, 1)
                pre(dve.reciprocal(degree[:], root[:]))
                pre(dve.tensor_tensor(z.dinv[:], degree[:], above[:], ALU.mult))
                with dve.Fori(0, steps) as i:
                    link = Link(dve, links, pre.n + i * L)
                    tiles = bass.ds(i * B7, B7)
                    link(dve.scalar_tensor_tensor(out=act7[:], in0=z.SUM[:, tiles, :], scalar=SLOPE,
                                                  in1=z.SUM[:, tiles, :], op0=ALU.mult, op1=ALU.max))
                    link(dve.tensor_tensor(z.X[:, tiles, :], z.X[:, tiles, :], act7[:], ALU.add))
                    norm_relu(dve, link, var_ready, std_ready, i + 1, z.X[:, tiles, :], h[:], b)
                    dve.sem_inc(h_ready, 1)
                    dve.wait_ge(m_ready, i + 1)
                    link(dve.tensor_tensor(z.H[:, tiles, :], psM[:, 0:B7, :], bcast(z.dinv[:, tiles], C), ALU.mult))
                    dve.sem_inc(tab_ready, 1)

            @block.scalar
            def _(act):
                act.wait_ge(degree_ready, 1)
                act.activation(root[:], degree[:], ACT.Sqrt).then_inc(root_ready, 1)
                with act.Fori(0, steps) as i:
                    act_root(act, z, b, var_ready, std_ready, i + 1)
                    act.wait_ge(t_ready, i + 1)
                    act.activation(hT[:], psT[:, 0:B7, :], ACT.Copy).then_inc(hT_ready, 1)

            @block.tensor
            def _(pe):
                pe.wait_ge(w_in, 16)
                with pe.Fori(0, steps) as i:
                    pe.wait_ge(h_ready, i + 1)
                    for j in range(B7):
                        ins = pe.transpose(psT[:, j, :], h[:, j, :], z.ident[:])
                    ins.then_inc(t_ready, 1)
                    pe.wait_ge(hT_ready, i + 1)
                    for j in range(B7):
                        ins = pe.matmul(psM[:, j, :], hT[:, j, :], ws[:], start=True, stop=True)
                    ins.then_inc(m_ready, 1)


def finish(nc, z, out, bias):
    A = z.A
    steps = A // B7
    with ExitStack() as ctx:
        m = Mem(nc, ctx, "finish")
        brow = m.sb("bias", [P, C])
        b_in, links, out_ready, out_done = m.sem("b_in"), m.sem("links"), m.sem("out_ready"), m.sem("out_done")
        full = z.N // P
        rest = z.N - full * P
        with nc.Block() as block:
            @block.sync
            def _(sp):
                sp.dma_start(brow[:], bias.partition_broadcast(P)).then_inc(b_in, 16)
                sp.wait_ge(out_ready, 1)
                sp.dma_start(out[0:full * P, :].rearrange("(a p) f -> p a f", p=P), z.X[:, 0:full, :]
                             ).then_inc(out_done, 16)
                sp.dma_start(out[full * P:z.N, :], z.X[0:rest, full, :]).then_inc(out_done, 16)
                sp.wait_ge(out_done, 32)

            @block.vector
            def _(dve):
                link = Link(dve, links)
                dve.wait_ge(b_in, 16)
                link(dve.tensor_tensor(z.SUM[:], z.SUM[:], z.H[:], ALU.add))
                link(dve.tensor_tensor(z.SUM[:], z.SUM[:], bcast(z.dinv[:], C), ALU.mult))
                link(dve.tensor_tensor(z.X[:], z.X[:], bcast_mid(brow[:], A), ALU.add))
                dve.tensor_tensor(z.X[:], z.X[:], z.SUM[:], ALU.add).then_inc(out_ready, 1)




def query_sums(nc, z, tabQ, tabQsum, scratch):
    A, NG = z.A, z.NG
    F = 5
    with ExitStack() as ctx:
        m = Mem(nc, ctx, "query_sums")
        key_i, digit_i = m.sb("key_i", [P, z.T], I32), m.sb("digit_i", [P, z.T], I32)
        tiles_row = m.sb("tiles_row", [P, A])
        stage = m.sb("stage", [P, 2, G], I32)
        rows = m.sb("rows", [P, 2, G, F])
        low = m.sb("low_onehot", [P, 2, G, P])
        high = m.sb("high_onehot", [P, 2, G, A])
        prod = m.sb("prod", [P, 2, G, A * F])
        sums = m.sb("sums", [P, A, F])
        below = m.sb("below", [P, P])
        total = m.sb("total", [P, A])
        one_a = m.sb("one_a", [P, A])
        cum = m.sb("cum", [P, A])
        counts = m.sb("counts", [P, A])
        acc = m.psum("acc", [P, A * F])
        ps = m.psum("prefix", [P, 2, A])
        gathered = [m.sem(f"gathered{q}") for q in range(2)]
        consts, links, staged, waited = m.sem("consts"), m.sem("links"), m.sem("staged"), m.sem("waited")
        onehots, prod_ready, used, sums_ready = m.sem("onehots"), m.sem("prod_ready"), m.sem("used"), m.sem("sums_ready")
        acc_ready = m.sem("acc_ready")
        counts_ready, prefix_ready, sums_out = m.sem("counts_ready"), m.sem("prefix_ready"), m.sem("sums_out")

        def pairs(eng, body):
            body(0, 0)
            body(1, 1)
            with eng.Fori(1, NG // 2) as i:
                body(2 * i, 0)
                body(2 * i + 1, 1)

        with nc.Block() as block:
            @block.gpsimd
            def _(pool):
                pool.iota(tiles_row[:], [[1, A]], base=0, channel_multiplier=0,
                          allow_small_or_imprecise_dtypes=True).then_inc(consts, 1)
                pool.memset(rows[:], 1.0).then_inc(consts, 1)
                pool.memset(one_a[:], 1.0).then_inc(consts, 1)
                pool.affine_select(out=below[:], in_=z.ones[:], compare_op=ALU.is_gt, fill=0.0, base=0,
                                   pattern=[[1, P]], channel_multiplier=-1).then_inc(consts, 1)
                pool.wait_ge(consts, 4)

                def gathers(g, q):
                    pool.wait_ge(staged, g + 1)
                    pool.sem_inc(waited, 1)
                    for j in range(G):
                        pool.indirect_dma_start(rows[:, q, j, 0:4], None, tabQ,
                                                bass.IndirectOffsetOnAxis(ap=stage[:, q, j:j + 1], axis=0),
                                                ).then_inc(gathered[q], 16)
                pairs(pool, gathers)

            @block.scalar
            def _(act):
                def indices(g, q):
                    if not (isinstance(g, int) and g < 2):
                        act.wait_ge(prod_ready, g - 1)
                    act.activation(stage[:, q, :], z.dstI[:, bass.ds(g * G, G)], ACT.Copy).then_inc(staged, 1)
                pairs(act, indices)

            @block.vector
            def _(dve):
                link = Link(dve, links)
                link(dve.tensor_copy(key_i[:], z.srcF[:]))
                link(dve.tensor_scalar(digit_i[:], key_i[:], 7, None, ALU.arith_shift_right))
                link(dve.tensor_copy(z.srcHigh[:], digit_i[:]))
                link(dve.tensor_scalar(key_i[:], key_i[:], P - 1, None, ALU.bitwise_and))
                link(dve.tensor_copy(z.srcLow[:], key_i[:]))
                dve.wait_ge(consts, 4)

                def products(g, q):
                    if not (isinstance(g, int) and g < 2):
                        dve.wait_ge(used, g - 1)
                    cols = bass.ds(g * G, G)
                    dve.tensor_tensor(low[:, q, :, :], bcast(z.srcLow[:, cols], P), bcast_mid(z.iota[:], G),
                                      ALU.is_equal)
                    dve.tensor_tensor(high[:, q, :, :], bcast(z.srcHigh[:, cols], A), bcast_mid(tiles_row[:], G),
                                      ALU.is_equal).then_inc(onehots, 1)
                    dve.wait_ge(onehots, g + 1)
                    dve.wait_ge(gathered[q], (g // 2 + 1) * G * 16 if isinstance(g, int) else (g + (2 - q)) * (G * 8))
                    for j in range(G):
                        ins = dve.tensor_tensor(
                            prod[:, q, j, :].rearrange("p (a f) -> p a f", f=F), bcast(high[:, q, j, :], F),
                            bcast_mid(rows[:, q, j, :], A), ALU.mult)
                    ins.then_inc(prod_ready, 1)
                pairs(dve, products)
                dve.wait_ge(acc_ready, 1)
                link(dve.tensor_copy(sums[:], acc[:].rearrange("p (a f) -> p a f", f=F)))
                dve.sem_inc(sums_ready, 1)
                dve.tensor_copy(counts[:], sums[:, :, 4]).then_inc(counts_ready, 1)
                dve.wait_ge(prefix_ready, 1)
                link(dve.tensor_copy(total[:], ps[:, 1, :]))
                link(dve.tensor_tensor_scan(cum[:], one_a[:], total[:], 0.0, ALU.mult, ALU.add))
                link(dve.tensor_tensor(cum[:], cum[:], total[:], ALU.subtract))
                dve.tensor_tensor(z.first[:], cum[:], ps[:, 0, :], ALU.add)

            @block.tensor
            def _(pe):
                pe.matmul(acc[:], z.zero16[:, 0:P], z.zero_wide[:, 0:A * F], start=True, stop=False)

                def products(g, q):
                    pe.wait_ge(prod_ready, g + 1)
                    for j in range(G):
                        ins = pe.matmul(acc[:], low[:, q, j, :], prod[:, q, j, :], start=False, stop=False)
                    ins.then_inc(used, 1)
                pairs(pe, products)
                pe.matmul(acc[:], z.zero16[:, 0:P], z.zero_wide[:, 0:A * F], start=False, stop=True
                          ).then_inc(acc_ready, 1)
                pe.wait_ge(counts_ready, 1)
                pe.matmul(ps[:, 0, :], below[:], counts[:], start=True, stop=True)
                pe.matmul(ps[:, 1, :], z.ones[:], counts[:], start=True, stop=True).then_inc(prefix_ready, 1)

            @block.sync
            def _(sp):
                sp.wait_ge(sums_ready, 1)
                sp.dma_start(node_rows(tabQsum, 0, A), sums[:, :, 0:4]).then_inc(sums_out, 16)
                sp.wait_ge(sums_out, 16)


def sort_by_source(nc, z, sorted_edges):
    A, NG = z.A, z.NG
    with ExitStack() as ctx:
        m = Mem(nc, ctx, "sort")
        tiles_row = m.sb("tiles_row", [P, A])
        earlier = m.sb("earlier", [P, P])
        low, lowT = m.sb("low", [P, 2, G, P]), m.sb("lowT", [P, 2, G, P])
        high = m.sb("high", [P, 2, G, A])
        key = m.sb("key", [P, 2, G])
        record = m.sb("record", [P, 2, G, 2], I32)
        running = m.sb("running", [P, A])
        picked, same = m.sb("picked", [P, 2, G, A]), m.sb("same", [P, 2, G, P])
        base, within = m.sb("base", [P, 2, G]), m.sb("within", [P, 2, G])
        rank = m.sb("rank", [P, 2, G], I32)
        psT, psK = m.psum("psT", [P, G, P]), m.psum("psK", [P, 2, G, P])
        psG = m.psum("psG", [P, 2, G, P])
        psR = m.psum("psR", [P, A])
        consts, onehots, turned, keys_turned = m.sem("consts"), m.sem("onehots"), m.sem("turned"), m.sem("keys_turned")
        lowT_ready, counted, running_ready = m.sem("lowT_ready"), m.sem("counted"), m.sem("running_ready")
        sums_ready, rank_ready, waited = m.sem("sums_ready"), m.sem("rank_ready"), m.sem("waited")
        scattered = [m.sem(f"scattered{q}") for q in range(2)]

        def pairs(eng, body):
            body(0, 0)
            body(1, 1)
            with eng.Fori(1, NG // 2) as i:
                body(2 * i, 0)
                body(2 * i + 1, 1)

        def early(g):
            return isinstance(g, int) and g < 2

        with nc.Block() as block:
            @block.gpsimd
            def _(pool):
                pool.iota(tiles_row[:], [[1, A]], base=0, channel_multiplier=0,
                          allow_small_or_imprecise_dtypes=True).then_inc(consts, 1)
                pool.affine_select(out=earlier[:], in_=z.ones[:], compare_op=ALU.is_gt, fill=0.0, base=0,
                                   pattern=[[-1, P]], channel_multiplier=1).then_inc(consts, 1)

                def scatter(g, q):
                    pool.wait_ge(rank_ready, g + 1)
                    pool.sem_inc(waited, 1)
                    for j in range(G):
                        pool.indirect_dma_start(sorted_edges,
                                                bass.IndirectOffsetOnAxis(ap=rank[:, q, j:j + 1], axis=0),
                                                record[:, q, j, :], None).then_inc(scattered[q], 16)
                pairs(pool, scatter)
                for q in range(2):
                    pool.wait_ge(scattered[q], NG // 2 * G * 16)

            @block.vector
            def _(dve):
                dve.wait_ge(consts, 2)

                def one_hots(g, q):
                    if not early(g):
                        dve.wait_ge(counted, g * G - G)
                        dve.wait_ge(keys_turned, g - 1)
                        dve.wait_ge(scattered[q], (g - q) * (G * 8))
                    cols = bass.ds(g * G, G)
                    dve.tensor_copy(key[:, q, :], z.srcF[:, cols])
                    dve.tensor_copy(record[:, q, :, 0], z.srcI[:, cols])
                    dve.tensor_copy(record[:, q, :, 1], z.dstI[:, cols])
                    dve.tensor_tensor(low[:, q, :, :], bcast(z.srcLow[:, cols], P), bcast_mid(z.iota[:], G),
                                      ALU.is_equal)
                    dve.tensor_tensor(high[:, q, :, :], bcast(z.srcHigh[:, cols], A), bcast_mid(tiles_row[:], G),
                                      ALU.is_equal).then_inc(onehots, 1)

                def ranks(g, q):
                    dve.wait_ge(keys_turned, g + 1)
                    dve.wait_ge(counted, g * G + G)
                    for j in range(G):
                        dve.scalar_tensor_tensor(out=same[:, q, j, :], in0=psK[:, q, j, :], scalar=key[:, q, j:j + 1],
                                                 in1=earlier[:], op0=ALU.is_equal, op1=ALU.mult,
                                                 accum_out=within[:, q, j:j + 1])
                        ins = dve.scalar_tensor_tensor(out=picked[:, q, j, :], in0=psG[:, q, j, 0:A], scalar=1.0,
                                                       in1=high[:, q, j, :], op0=ALU.mult, op1=ALU.mult,
                                                       accum_out=base[:, q, j:j + 1])
                    ins.then_inc(sums_ready, 1)
                    dve.wait_ge(sums_ready, g + 1)
                    dve.tensor_tensor(rank[:, q, :], base[:, q, :], within[:, q, :], ALU.add).then_inc(rank_ready, 1)

                one_hots(0, 0)
                one_hots(1, 1)
                ranks(0, 0)
                with dve.Fori(1, NG // 2) as i:
                    one_hots(2 * i, 0)
                    ranks(2 * i - 1, 1)
                    one_hots(2 * i + 1, 1)
                    ranks(2 * i, 0)
                ranks(NG - 1, 1)

            @block.scalar
            def _(act):
                def turn(g, q):
                    act.wait_ge(turned, g + 1)
                    act.activation(lowT[:, q, :, :], psT[:], ACT.Copy).then_inc(lowT_ready, 1)
                    for j in range(G):
                        act.wait_ge(counted, g * G + (j + 1))
                        act.activation(running[:], psR[:], ACT.Copy).then_inc(running_ready, 1)
                act.activation(running[:], z.first[:], ACT.Copy).then_inc(running_ready, 1)
                pairs(act, turn)

            @block.tensor
            def _(pe):
                def chunk(g, q):
                    pe.wait_ge(onehots, g + 1)
                    if isinstance(g, int) and g < 1:
                        pass
                    else:
                        pe.wait_ge(lowT_ready, g)
                    for j in range(G):
                        ins = pe.transpose(psT[:, j, :], low[:, q, j, :], z.ident[:])
                    ins.then_inc(turned, 1)
                    if not early(g):
                        pe.wait_ge(rank_ready, g - 1)
                    for j in range(G):
                        ins = pe.transpose(psK[:, q, j, :], key[:, q, j:j + 1].to_broadcast([P, P]), z.ident[:])
                    ins.then_inc(keys_turned, 1)
                    pe.wait_ge(lowT_ready, g + 1)
                    for j in range(G):
                        pe.wait_ge(running_ready, g * G + (j + 1))
                        pe.matmul(psG[:, q, j, 0:A], lowT[:, q, j, :], running[:], start=True, stop=True)
                        pe.matmul(psR[:], z.ident[:], running[:], start=True, stop=False)
                        pe.matmul(psR[:], low[:, q, j, :], high[:, q, j, :], start=False, stop=True
                                  ).then_inc(counted, 1)
                pairs(pe, chunk)


def edge_scores(nc, z, sorted_edges, tabK, tabQsum, scores, edges):
    NG = z.NG
    with ExitStack() as ctx:
        m = Mem(nc, ctx, "scores")
        stage = m.sb("stage", [P, 2, G, 2], I32)
        rows = m.sb("rows", [P, 2, G, 2, 4])
        gathered = [m.sem(f"gathered{q}") for q in range(2)]
        edges_in, staged, waited, multiplied = m.sem("edges_in"), m.sem("staged"), m.sem("waited"), m.sem("multiplied")

        def pairs(eng, body):
            body(0, 0)
            body(1, 1)
            with eng.Fori(1, NG // 2) as i:
                body(2 * i, 0)
                body(2 * i + 1, 1)

        with nc.Block() as block:
            @block.sync
            def _(sp):
                sp.dma_start(edges[:], sorted_edges.rearrange("(p j) k -> p j k", p=P)).then_inc(edges_in, 16)

            @block.scalar
            def _(act):
                act.wait_ge(edges_in, 16)

                def indices(g, q):
                    if not (isinstance(g, int) and g < 2):
                        act.wait_ge(multiplied, g - 1)
                    act.activation(stage[:, q, :, :], edges[:, bass.ds(g * G, G), :], ACT.Copy).then_inc(staged, 1)
                pairs(act, indices)

            @block.gpsimd
            def _(pool):
                def gathers(g, q):
                    pool.wait_ge(staged, g + 1)
                    pool.sem_inc(waited, 1)
                    for j in range(G):
                        for side, table in ((0, tabK), (1, tabQsum)):
                            pool.indirect_dma_start(rows[:, q, j, side, :], None, table,
                                                    bass.IndirectOffsetOnAxis(ap=stage[:, q, j, side:side + 1], axis=0),
                                                    ).then_inc(gathered[q], 16)
                pairs(pool, gathers)

            @block.vector
            def _(dve):
                def multiply(g, q):
                    dve.wait_ge(gathered[q], (g // 2 + 1) * 2 * G * 16 if isinstance(g, int) else (g + (2 - q)) * (G * 16))
                    dve.tensor_tensor(scores[:, bass.ds(g * G, G), :], rows[:, q, :, 0, :], rows[:, q, :, 1, :],
                                      ALU.mult).then_inc(multiplied, 1)
                pairs(dve, multiply)


def edge_softmax(nc, z, scores, edges, flat):
    T, H, BIG = z.T, 4, 3.0e38
    with ExitStack() as ctx:
        m = Mem(nc, ctx, "softmax")
        src, dst = m.sb("src", [P, T]), m.sb("dst", [P, T])
        same_prev, same_next = m.sb("same_prev", [P, T]), m.sb("same_next", [P, T])
        pen_prev, pen_next = m.sb("pen_prev", [P, T]), m.sb("pen_next", [P, T])
        fwd, bwd, tmp = m.sb("fwd", [P, T]), m.sb("bwd", [P, T]), m.sb("tmp", [P, T])
        weight = m.sb("weight", [P, T])
        ends = m.sb("ends", [P, 2, H])
        key_rows = m.sb("key_rows", [H, 2, P + 1])
        joined, pen_row = m.sb("joined", [H, 2, P]), m.sb("pen_row", [H, 2, P])
        neighbour = m.sb("neighbour", [P, 2, H])
        col = m.sb("col", [P, H])
        row, chain = m.sb("row", [H, P]), m.sb("chain", [H, P + 1])
        carry = m.sb("carry", [P, H])
        psR, psC = m.psum("psR", [H, 2, P]), m.psum("psC", [P, 2, H])
        psr, psc = m.psum("psr", [H, P]), m.psum("psc", [P, H])
        links, ends_ready, rows_ready, shifted, cols_ready = (m.sem(s) for s in (
            "links", "ends_ready", "rows_ready", "shifted", "cols_ready"))
        col_ready, row_ready, chain_ready, carry_ready = (m.sem(s) for s in (
            "col_ready", "row_ready", "chain_ready", "carry_ready"))
        less_max, powers_ready, weight_ready, flat_out = (m.sem(s) for s in (
            "less_max", "powers_ready", "weight_ready", "flat_out"))
        CHAINS = 4
        with nc.Block() as block:
            @block.vector
            def _(dve):
                link = Link(dve, links)
                link(dve.tensor_copy(src[:], edges[:, :, 0]))
                link(dve.tensor_copy(dst[:], edges[:, :, 1]))
                for h in range(H):
                    link(dve.tensor_copy(ends[:, 0, h:h + 1], src[:, T - 1:T]))
                    link(dve.tensor_copy(ends[:, 1, h:h + 1], src[:, 0:1]))
                dve.sem_inc(ends_ready, 1)
                link(dve.memset(key_rows[:], -1.0))
                dve.wait_ge(rows_ready, 1)
                link(dve.tensor_copy(key_rows[:, 0, 1:P + 1], psR[:, 0, :]))
                link(dve.tensor_copy(key_rows[:, 1, 0:P], psR[:, 1, :]))
                dve.sem_inc(shifted, 1)
                for d in range(2):
                    link(dve.tensor_tensor(joined[:, d, :], key_rows[:, d, 1:P + 1], key_rows[:, d, 0:P], ALU.is_equal))
                    link(dve.tensor_scalar(pen_row[:, d, :], joined[:, d, :], -1.0, BIG, ALU.add, ALU.mult))
                dve.wait_ge(cols_ready, 1)
                link(dve.tensor_copy(neighbour[:], psC[:]))
                link(dve.tensor_tensor(same_prev[:, 1:T], src[:, 1:T], src[:, 0:T - 1], ALU.is_equal))
                link(dve.tensor_tensor(same_prev[:, 0:1], src[:, 0:1], neighbour[:, 0, 0:1], ALU.is_equal))
                link(dve.tensor_copy(same_next[:, 0:T - 1], same_prev[:, 1:T]))
                link(dve.tensor_tensor(same_next[:, T - 1:T], src[:, T - 1:T], neighbour[:, 1, 0:1], ALU.is_equal))
                link(dve.tensor_scalar(pen_prev[:], same_prev[:], -1.0, BIG, ALU.add, ALU.mult))
                link(dve.tensor_scalar(pen_next[:], same_next[:], -1.0, BIG, ALU.add, ALU.mult))
                used = [0]

                def chained(direction, mask_row, identity, op0, op1):
                    used[0] += 1
                    dve.sem_inc(col_ready, 1)
                    link(dve.memset(chain[:], identity))
                    dve.wait_ge(row_ready, used[0])
                    link(dve.tensor_copy(row[:], psr[:]))
                    if direction == 0:
                        link(dve.tensor_tensor_scan(chain[:, 1:P + 1], mask_row, row[:], identity, op0, op1))
                    else:
                        link(dve.tensor_tensor_scan(chain[:, P - 1::-1], mask_row[:, ::-1], row[:, ::-1], identity,
                                                    op0, op1))
                    dve.sem_inc(chain_ready, 1)
                    dve.wait_ge(carry_ready, used[0])
                    link(dve.tensor_copy(carry[:], psc[:]))

                def forward_max(h, init):
                    link(dve.tensor_tensor_scan(fwd[:], pen_prev[:], scores[:, :, h], init, ALU.add, ALU.max))

                def backward_max(h, init):
                    link(dve.tensor_tensor_scan(bwd[:, ::-1], pen_next[:, ::-1], fwd[:, ::-1], init, ALU.add, ALU.max))

                def forward_sum(h, init):
                    link(dve.tensor_tensor_scan(fwd[:], same_prev[:], scores[:, :, h], init, ALU.mult, ALU.add))

                def backward_sum(h, init):
                    link(dve.tensor_tensor(tmp[:], fwd[:], same_next[:], ALU.mult))
                    link(dve.tensor_tensor(tmp[:], fwd[:], tmp[:], ALU.subtract))
                    link(dve.tensor_tensor_scan(bwd[:, ::-1], same_next[:, ::-1], tmp[:, ::-1], init, ALU.mult, ALU.add))

                carry_f = m.sb("carry_f", [P, 2, H])
                for kind, (forward, backward, ident_f, op0, op1, masks) in enumerate((
                        (forward_max, backward_max, -BIG, ALU.add, ALU.max, pen_row),
                        (forward_sum, backward_sum, 0.0, ALU.mult, ALU.add, joined))):
                    if kind == 1:
                        dve.wait_ge(powers_ready, 1)
                    for h in range(H):
                        forward(h, ident_f)
                        link(dve.tensor_copy(col[:, h:h + 1], fwd[:, T - 1:T]))
                    chained(0, masks[:, 0, :], ident_f, op0, op1)
                    link(dve.tensor_copy(carry_f[:, kind, :], carry[:]))
                    for h in range(H):
                        forward(h, carry_f[:, kind, h:h + 1])
                        backward(h, ident_f)
                        link(dve.tensor_copy(col[:, h:h + 1], bwd[:, 0:1]))
                    chained(1, masks[:, 1, :], ident_f, op0, op1)
                    for h in range(H):
                        forward(h, carry_f[:, kind, h:h + 1])
                        backward(h, carry[:, h:h + 1])
                        if kind == 0:
                            link(dve.tensor_tensor(scores[:, :, h], scores[:, :, h], bwd[:], ALU.subtract))
                        else:
                            link(dve.tensor_scalar(bwd[:], bwd[:], 1e-8, None, ALU.add))
                            link(dve.reciprocal(tmp[:], bwd[:]))
                            link(dve.tensor_tensor(tmp[:], scores[:, :, h], tmp[:], ALU.mult))
                            if h == 0:
                                link(dve.tensor_copy(weight[:], tmp[:]))
                            else:
                                link(dve.tensor_tensor(weight[:], weight[:], tmp[:], ALU.add))
                    if kind == 0:
                        dve.sem_inc(less_max, 1)
                dve.tensor_scalar(weight[:], weight[:], 1.0 / H, None, ALU.mult).then_inc(weight_ready, 1)

            @block.scalar
            def _(act):
                act.wait_ge(less_max, 1)
                act.activation(scores[:], scores[:], ACT.Exp).then_inc(powers_ready, 1)

            @block.tensor
            def _(pe):
                pe.wait_ge(ends_ready, 1)
                pe.transpose(psR[:, 0, :], ends[:, 0, :], z.ident[:])
                pe.transpose(psR[:, 1, :], ends[:, 1, :], z.ident[:]).then_inc(rows_ready, 1)
                pe.wait_ge(shifted, 1)
                pe.transpose(psC[:, 0, :], key_rows[:, 0, 0:P], z.ident[0:H, 0:H])
                pe.transpose(psC[:, 1, :], key_rows[:, 1, 1:P + 1], z.ident[0:H, 0:H]).then_inc(cols_ready, 1)
                for n in range(CHAINS):
                    pe.wait_ge(col_ready, n + 1)
                    pe.transpose(psr[:], col[:], z.ident[:]).then_inc(row_ready, 1)
                    pe.wait_ge(chain_ready, n + 1)
                    shown = chain[:, 0:P] if n % 2 == 0 else chain[:, 1:P + 1]
                    pe.transpose(psc[:], shown, z.ident[0:H, 0:H]).then_inc(carry_ready, 1)

            @block.sync
            def _(sp):
                sp.wait_ge(weight_ready, 1)
                for array, held in zip(flat, (src, dst, weight)):
                    sp.dma_start(array.rearrange("(p j) -> p j", p=P), held[:]).then_inc(flat_out, 16)
                sp.wait_ge(flat_out, 48)


def load_sorted(nc, z, flat, keyF, indexI, weightF):
    T, K = z.T, z.K
    fk, fr = T // P, T % P
    with ExitStack() as ctx:
        m = Mem(nc, ctx, "load_sorted")
        rows = [m.sb(f"rows{i}", [P, K, P]) for i in range(3)]
        index_f = m.sb("index_f", [P, T])
        turned = [m.psum(f"turned{i}", [P, 4 * 512]) for i in range(2)]
        rows_in, rows_turned, lists_out = m.sem("rows_in"), m.sem("rows_turned"), m.sem("lists_out")
        with nc.Block() as block:
            @block.sync
            def _(sp):
                for array, r in zip(flat, rows):
                    sp.dma_start(r[:, 0:fk, :], array[0:fk * P * P].rearrange("(k r c) -> r k c", r=P, c=P)
                                 ).then_inc(rows_in, 16)
                    sp.dma_start(r[0:fr, fk, :], array[fk * P * P:T * P].rearrange("(r c) -> r c", c=P)
                                 ).then_inc(rows_in, 16)

            @block.vector
            def _(dve):
                for i, out in enumerate((keyF, index_f, weightF)):
                    dve.wait_ge(rows_turned, i + 1)
                    for b in range(0, T, 512):
                        n = min(512, T - b)
                        ins = dve.tensor_copy(out[:, b:b + n], turned[i % 2][:, b:b + n])
                    ins.then_inc(lists_out, 1)
                dve.wait_ge(lists_out, 3)
                dve.tensor_copy(indexI[:], index_f[:])

            @block.tensor
            def _(pe):
                pe.wait_ge(rows_in, 6 * 16)
                for i in range(3):
                    if i == 2:
                        pe.wait_ge(lists_out, 1)
                    for k in range(K):
                        n = min(P, T - k * P)
                        ins = pe.transpose(turned[i % 2][:, k * P:k * P + n], rows[i][0:n, k, :], z.ident[0:n, 0:n])
                    ins.then_inc(rows_turned, 1)


def program(nc, x, src, dst, weight, w1, b1, g1, be1, w2, b2, g2, be2,
            sw1l, sb1, sw1r, sw2l, sb2, sw2r, wq, wk, wo, bo, gw, gb, out):
    z = Sizes(x.shape[0], src.shape[0])
    with ExitStack() as ctx:
        persist = Mem(nc, ctx, "kept")

        def dram(name, shape, dt=F32):
            return nc.dram_tensor(name, shape, dt, kind="Internal").ap()

        tabA, tabB, tabH, tabH2, tabV, tabX = (dram(n, (z.NP, C)) for n in ("tabA", "tabB", "tabH", "tabH2", "tabV", "tabX"))
        tabQ, tabK = dram("tabQ", (z.NP, 4)), dram("tabK", (z.NP, 4))
        msg = dram("msg", (z.EP, C))
        tabQsum, sorted_edges = dram("tabQsum", (z.NP, 4)), dram("sorted_edges", (z.EP, 2), I32)
        flat = [dram(n, (z.EP,)) for n in ("sorted_src", "sorted_dst", "sorted_weight")]
        make_constants(nc, z, persist)
        load_edge_lists(nc, z, persist, src, dst, weight)
        z.dst_windows = find_windows(nc, z, persist, z.dstF, "dst", dram("dst_ends", (z.A, 2)))
        z.X = persist.sb("X", [P, z.A, C])
        z.SUMX = persist.sb("SUMX", [P, z.A, 2])
        z.rcount = persist.sb("rcount", [P, z.A])
        z.dinv = persist.sb("dinv", [P, z.A])
        with ExitStack() as part:
            held = Mem(nc, part, "first")
            z.H = held.sb("H", [P, z.A, C])
            z.SUM = held.sb("SUM", [P, z.A, C])
            entry(nc, z, x, tabA, tabB, w1, b1)
            edge_mlp(nc, z, tabA, tabB, msg, w2, b2, g1, be1, g2, be2)
            segment_sum(nc, z, "sum_mlp", z.dst_windows, z.dstF, z.SUM, rows=msg, scale=z.one_w[:, :, 1])
            after_mlp(nc, z, tabH)
            segment_sum(nc, z, "sum_sage1", z.dst_windows, z.dstF, z.SUM, gather=(tabH, z.srcI), extras=z.one_w,
                        extras_out=z.SUMX)
            sage_layer(nc, z, "sage1", sw1l, sb1, sw1r, hidden_table=tabH2)
            segment_sum(nc, z, "sum_sage2", z.dst_windows, z.dstF, z.SUM, gather=(tabH2, z.srcI))
            sage_layer(nc, z, "sage2", sw2l, sb2, sw2r, attention=(wq, wk, wo, bo, tabQ, tabK, tabV))
        with ExitStack() as part:
            held = Mem(nc, part, "sorting")
            z.srcHigh, z.srcLow = held.sb("srcHigh", [P, z.T]), held.sb("srcLow", [P, z.T])
            z.first = held.sb("first_rank", [P, z.A])
            query_sums(nc, z, tabQ, tabQsum, None)
            sort_by_source(nc, z, sorted_edges)
        with ExitStack() as part:
            held = Mem(nc, part, "softmaxing")
            scores = held.sb("scores", [P, z.T, 4])
            edges = held.sb("edges", [P, z.T, 2], I32)
            edge_scores(nc, z, sorted_edges, tabK, tabQsum, scores, edges)
            edge_softmax(nc, z, scores, edges, flat)
        with ExitStack() as part:
            held = Mem(nc, part, "second")
            z.H = held.sb("H", [P, z.A, C])
            z.SUM = held.sb("SUM", [P, z.A, C])
            with ExitStack() as inner:
                lists = Mem(nc, inner, "by_source")
                keyF, weightF = lists.sb("keyF", [P, z.T]), lists.sb("weightF", [P, z.T])
                indexI = lists.sb("indexI", [P, z.T], I32)
                load_sorted(nc, z, flat, keyF, indexI, weightF)
                windows = find_windows(nc, z, lists, keyF, "src", dram("src_ends", (z.A, 2)))
                segment_sum(nc, z, "sum_attention", windows, keyF, z.SUM, gather=(tabV, indexI), scale=weightF)
            after_attention(nc, z, tabX, gw)
            segment_sum(nc, z, "sum_gcn", z.dst_windows, z.dstF, z.SUM, gather=(tabX, z.srcI),
                        scale=z.one_w[:, :, 1])
            finish(nc, z, out, gb)


_INS = (["x", "src", "dst", "edge_weight"] + ["L0_gnn_" + k for k in ("w1", "b1", "g1", "be1", "w2", "b2", "g2", "be2")]
        + ["L1_gnn_" + k for k in ("W1_l", "b1_l", "W1_r", "W2_l", "b2_l", "W2_r")]
        + ["L2_gnn_" + k for k in ("Wq", "Wk", "Wl", "bl")] + ["L3_gnn_W", "L3_gnn_b"])


def kernel(**inputs):
    import numpy as _np
    import concourse.bacc as _bacc
    from concourse import mybir as _mybir
    from concourse.bass_utils import run_bass_kernel_spmd as _run

    nc = _bacc.Bacc("TRN2", target_bir_lowering=False, num_devices=1)
    arrays, args = {}, []
    for name in _INS:
        a = _np.ascontiguousarray(inputs[name])
        arrays[f"in_{name}_dram"] = a
        args.append(nc.dram_tensor(f"in_{name}_dram", a.shape, _mybir.dt.from_np(a.dtype), kind="ExternalInput").ap())
    out = nc.dram_tensor("out_0_dram", inputs["x"].shape, F32, kind="ExternalOutput").ap()
    program(nc, *args, out)
    r = _run(nc, [arrays], core_ids=[0])
    return r.results[0]["out_0_dram"]
```

```python
from contextlib import ExitStack

import numpy as np
import concourse.bass as bass
from concourse import mybir

ALU = mybir.AluOpType
ACT = mybir.ActivationFunctionType
AX_X = mybir.AxisListType.X
F32 = mybir.dt.float32
BF16 = mybir.dt.bfloat16
I32 = mybir.dt.int32

P = 128
C = 128
G = 4
S = 2 * G
B7 = 7
EPS = 1e-5
IN_TILES = "a visit's tile lies between the lowest and the highest tile of keys below the number of nodes"
SLOPE = 0.2


class Link:

    def __init__(self, eng, sem, base=0):
        self.eng, self.sem, self.base, self.n = eng, sem, base, 0

    def __call__(self, ins):
        self.n += 1
        ins.then_inc(self.sem, 1)
        self.eng.wait_ge(self.sem, self.base + self.n)


class Sizes:
    def __init__(self, n, e):
        self.N, self.E = n, e
        self.A = -(-n // P)
        self.NP = self.A * P
        self.T = -(-e // (P * 2 * S)) * 2 * S
        self.NG = self.T // G
        self.NS = self.T // S
        self.EP = self.T * P
        self.K = -(-self.T // P)
        assert self.A % B7 == 0


class Mem:

    def __init__(self, nc, ctx, phase):
        self.nc, self.ctx, self.phase, self.sems = nc, ctx, phase, []
        ctx.callback(self.close)

    def sb(self, name, shape, dt=F32):
        return self.ctx.enter_context(self.nc.sbuf_tensor(f"{self.phase}_{name}", shape, dt))

    def psum(self, name, shape, dt=F32):
        return self.ctx.enter_context(self.nc.psum_tensor(f"{self.phase}_{name}", shape, dt))

    def sem(self, name):
        self.sems.append(self.nc.alloc_semaphore(f"{self.phase}_{name}"))
        return self.sems[-1]

    def close(self):
        if self.sems:
            self.nc.clear_and_free_semaphores(self.sems)
            self.nc.all_engine_barrier()


def bcast(ap, n):
    return ap.unsqueeze(2).to_broadcast([ap.shape[0], ap.shape[1], n])


def bcast_mid(ap, n):
    return ap.unsqueeze(1).to_broadcast([ap.shape[0], n, ap.shape[1]])


def node_rows(table, a0, n):
    return table[bass.ds(a0 * P, n * P), :].rearrange("(a p) f -> p a f", p=P)



def make_constants(nc, z, persist):
    k = persist
    z.ident = k.sb("ident", [P, P])
    z.iota = k.sb("iota_row", [P, P])
    z.tile_base = k.sb("tile_base", [P, z.A])
    z.ones = k.sb("ones", [P, P])
    z.zero16 = k.sb("zero16", [P, P], BF16)
    z.zero_wide = k.sb("zero_wide", [P, 512], BF16)
    z.eps = k.sb("eps_col", [P, 1])
    with ExitStack() as ctx:
        m = Mem(nc, ctx, "consts")
        ones_set = m.sem("ones_set")
        with nc.Block() as block:
            @block.gpsimd
            def _(pool):
                pool.memset(z.ones[:], 1.0).then_inc(ones_set, 1)
                pool.memset(z.zero16[:], 0.0)
                pool.memset(z.zero_wide[:], 0.0)
                pool.memset(z.eps[:], EPS)
                pool.iota(z.iota[:], [[1, P]], base=0, channel_multiplier=0, allow_small_or_imprecise_dtypes=True)
                pool.iota(z.tile_base[:], [[-P, z.A]], base=0, channel_multiplier=0,
                          allow_small_or_imprecise_dtypes=True)
                pool.wait_ge(ones_set, 1)
                pool.affine_select(out=z.ident[:], in_=z.ones[:], compare_op=ALU.is_equal, fill=0.0, base=0,
                                   pattern=[[-1, P]], channel_multiplier=1)



def load_edge_lists(nc, z, persist, src, dst, weight):
    T, K, E = z.T, z.K, z.E
    z.srcF = persist.sb("srcF", [P, T])
    z.dstF = persist.sb("dstF", [P, T])
    z.srcI = persist.sb("srcI", [P, T], I32)
    z.dstI = persist.sb("dstI", [P, T], I32)
    z.one_w = persist.sb("one_w", [P, T, 2])
    full = E // P
    tail = E - full * P
    fk = full // P
    fr = full - fk * P
    assert fk == K - 1 and tail > 0
    with ExitStack() as ctx:
        m = Mem(nc, ctx, "lists")
        rows_i = [m.sb(f"rows_i{i}", [P, K, P], I32) for i in range(2)]
        rows_w = m.sb("rows_w", [P, K, P])
        rows_f = [m.sb(f"rows_f{i}", [P, K, P]) for i in range(2)] + [rows_w]
        turned = [m.psum(f"turned{i}", [P, 4 * 512]) for i in range(2)]
        pads_set, rows_in = m.sem("pads_set"), m.sem("rows_in")
        rows_cast, rows_turned, lists_out = m.sem("rows_cast"), m.sem("rows_turned"), m.sem("lists_out")
        with nc.Block() as block:
            @block.gpsimd
            def _(pool):
                for r in rows_i:
                    pool.memset(r[:, K - 1, :], z.NP - 1).then_inc(pads_set, 1)
                pool.memset(rows_w[:, K - 1, :], 0.0).then_inc(pads_set, 1)
                pool.memset(z.one_w[:, :, 0], 1.0)

            @block.sync
            def _(sp):
                sp.wait_ge(pads_set, 3)
                for rows, flat in ((rows_i[0], src), (rows_i[1], dst), (rows_w, weight)):
                    sp.dma_start(rows[:, 0:fk, :], flat[0:fk * P * P].rearrange("(k r c) -> r k c", r=P, c=P)
                                 ).then_inc(rows_in, 16)
                    sp.dma_start(rows[0:fr, fk, :], flat[fk * P * P:full * P].rearrange("(r c) -> r c", c=P)
                                 ).then_inc(rows_in, 16)
                    sp.dma_start(rows[fr:fr + 1, fk, 0:tail], flat[full * P:E].rearrange("(r c) -> r c", r=1)
                                 ).then_inc(rows_in, 16)

            @block.vector
            def _(dve):
                dve.wait_ge(rows_in, 9 * 16)
                for i in range(2):
                    dve.tensor_copy(rows_f[i][:], rows_i[i][:]).then_inc(rows_cast, 1)
                outs = (z.srcF[:], z.dstF[:], z.one_w[:, :, 1])
                for i in range(3):
                    dve.wait_ge(rows_turned, i + 1)
                    for b in range(0, T, 512):
                        n = min(512, T - b)
                        ins = dve.tensor_copy(outs[i][:, b:b + n], turned[i % 2][:, b:b + n])
                    ins.then_inc(lists_out, 1)
                dve.wait_ge(lists_out, 3)
                dve.tensor_copy(z.srcI[:], z.srcF[:])
                dve.tensor_copy(z.dstI[:], z.dstF[:])

            @block.tensor
            def _(pe):
                pe.wait_ge(rows_cast, 2)
                for i in range(3):
                    if i == 2:
                        pe.wait_ge(lists_out, 1)
                    for q in range(K):
                        n = min(P, T - q * P)
                        ins = pe.transpose(turned[i % 2][:, q * P:q * P + n], rows_f[i][0:n, q, :],
                                           z.ident[0:n, 0:n])
                    ins.then_inc(rows_turned, 1)



def find_tiles(nc, z, persist, keyF, name):
    NS, T = z.NS, z.T
    table = persist.sb(f"{name}_visits", [1, NS * 4], I32)
    with ExitStack() as ctx:
        m = Mem(nc, ctx, f"{name}_tiles")
        key_i, tile_i = m.sb("key_i", [P, T], I32), m.sb("tile_i", [P, T], I32)
        tile_f = m.sb("tile_f", [P, T])
        ends = m.sb("ends", [P, 2, NS])
        ends_all = m.sb("ends_all", [P, 2, NS])
        one_row = m.sb("one_row", [1, NS])
        visits, after = m.sb("visits", [1, NS]), m.sb("after", [1, NS])
        table_f = m.sb("table_f", [1, NS, 4])
        links, ends_ready, ends_joined = m.sem("links"), m.sem("ends_ready"), m.sem("ends_joined")
        with nc.Block() as block:
            @block.vector
            def _(dve):
                link = Link(dve, links)
                link(dve.memset(one_row[:], 1.0))
                link(dve.memset(table_f[:], 0.0))
                link(dve.tensor_copy(key_i[:], keyF[:]))
                link(dve.tensor_scalar(tile_i[:], key_i[:], 7, None, ALU.arith_shift_right))
                link(dve.tensor_copy(tile_f[:], tile_i[:]))
                link(dve.tensor_reduce(ends[:, 0, :], tile_f[:].rearrange("p (g j) -> p g j", j=S), AX_X, ALU.max))
                link(dve.tensor_reduce(ends[:, 1, :], tile_f[:].rearrange("p (g j) -> p g j", j=S), AX_X, ALU.min))
                dve.tensor_scalar(ends[:, 1, :], ends[:, 1, :], -1.0, None, ALU.mult).then_inc(ends_ready, 1)
                dve.wait_ge(ends_joined, 1)
                link(dve.tensor_tensor(visits[:], ends_all[0:1, 0, :], ends_all[0:1, 1, :], ALU.add))
                link(dve.tensor_scalar(visits[:], visits[:], 1.0, None, ALU.add))
                link(dve.tensor_tensor_scan(after[:], one_row[:], visits[:], 0.0, ALU.mult, ALU.add))
                link(dve.tensor_tensor(table_f[:, :, 0], after[:], visits[:], ALU.subtract))
                link(dve.tensor_copy(table_f[:, :, 1], after[:]))
                link(dve.tensor_tensor(table_f[:, :, 2], table_f[:, :, 0], ends_all[0:1, 1, :], ALU.add))
                link(dve.tensor_scalar(table_f[:, :, 2], table_f[:, :, 2], -1.0, float(z.A * NS), ALU.mult, ALU.add))
                dve.tensor_copy(table[:], table_f[:].rearrange("o g k -> o (g k)"))

            @block.gpsimd
            def _(pool):
                pool.wait_ge(ends_ready, 1)
                pool.partition_all_reduce(ends_all[:].rearrange("p k g -> p (k g)"),
                                          ends[:].rearrange("p k g -> p (k g)"), P,
                                          bass.bass_isa.ReduceOp.max).then_inc(ends_joined, 1)
    return table


def unit_visits(nc, z, eng, table, at):
    top = z.A * z.NS
    _, (before, after, shift) = nc.values_load_multi_w_load_instructions(
        table[0:1, bass.ds(at, 3)], engines=[eng.engine], min_val=0, max_val=2 * top)
    return before, after, shift - top


def node_tile(nc, z, v, shift):
    return nc.s_assert_within(v + shift, 0, z.A - 1, skip_runtime_bounds_check_because=IN_TILES)


def pairs(z, eng, body, count=None):
    body(0, 0)
    body(1, 1)
    with eng.Fori(1, (count or z.NG) // 2) as i:
        body(2 * i, 0)
        body(2 * i + 1, 1)


def peeled(g):
    return isinstance(g, int) and g < 2


def parity_count(g, q):
    return (g - q) * 8 + 16



class Scatter:

    def __init__(self, nc, z, m, table, keyF, out, extras_out=None):
        self.nc, self.z, self.table, self.keyF, self.out, self.phase = nc, z, table, keyF, out, m.phase
        self.extras_out = extras_out
        self.width = C if extras_out is None else C + 2
        self.onehot = m.sb("onehot", [P, S, P])
        self.acc = m.psum("acc", [P, 2, 512])
        self.onehot_ready = m.sem("onehot_ready")
        self.product_done = m.sem("product_done")
        self.added = m.sem("added")
        self.finishing = m.sem("finishing")
        self.unit_done = m.sem("unit_done")

    def start_vector(self, dve):
        dve.sem_inc(self.added, 1)
        self.last_tile = dve.alloc_register(f"{self.phase}_last_tile")
        dve.reg_mov(self.last_tile, 0)

    def start_tensor(self, pe):
        for n in range(2):
            ins = pe.matmul(self.acc[:, n, 0:self.width], self.z.zero16[:, 0:P], self.z.zero_wide[:, 0:self.width],
                            start=True, stop=True)
        ins.then_inc(self.product_done, S)

    def add(self, dve, bank, tile):
        if self.extras_out is not None:
            x = self.extras_out[:, bass.ds(tile, 1), :]
            dve.tensor_tensor(x, x, self.acc[:, bass.ds(bank, 1), C:C + 2], ALU.add)
        x = self.out[:, bass.ds(tile, 1), :]
        dve.tensor_tensor(x, x, self.acc[:, bass.ds(bank, 1), 0:P], ALU.add).then_inc(self.added, 1)

    def vector(self, dve, first, at):
        before, after, shift = unit_visits(self.nc, self.z, dve, self.table, at)
        with dve.Fori(before, after) as v:
            a = node_tile(self.nc, self.z, v, shift)
            for j in range(S):
                dve.wait_ge(self.product_done, v * S + (j + 1))
                dve.tensor_scalar(self.onehot[:, j, :], self.z.iota[:], self.keyF[:, bass.ds(first + j, 1)],
                                  self.z.tile_base[:, bass.ds(a, 1)], ALU.subtract, ALU.is_equal
                                  ).then_inc(self.onehot_ready, 1)
            tile = dve.snap(self.last_tile, min_val=0, max_val=self.z.A - 1)
            dve.wait_ge(self.added, v + 1)
            self.add(dve, (v + 1) % 2, tile)
            dve.reg_mov(self.last_tile, a)

    def finish_vector(self, dve):
        last = dve.value_load(self.table[0:1, self.z.NS * 4 - 3:self.z.NS * 4 - 2], min_val=1,
                              max_val=self.z.A * self.z.NS)
        tile = dve.snap(self.last_tile, min_val=0, max_val=self.z.A - 1)
        dve.wait_ge(self.product_done, last * S + S)
        dve.sem_inc(self.finishing, 1)
        dve.wait_ge(self.added, last + 1)
        self.add(dve, (last + 1) % 2, tile)

    def tensor(self, pe, first, at, row, wait_row):
        before, after, shift = unit_visits(self.nc, self.z, pe, self.table, at)
        pe.wait_ge(self.product_done, before * S + S)
        pe.sem_inc(self.unit_done, 2)
        with pe.Fori(before, after) as v:
            bank = bass.ds(v % 2, 1)
            pe.wait_ge(self.added, v + 1)
            for j in range(S):
                wait_row(j)
                pe.wait_ge(self.onehot_ready, v * S + (j + 1))
                pe.matmul(self.acc[:, bank, 0:self.width], self.onehot[:, j, :], row(j), start=j == 0, stop=j == S - 1
                          ).then_inc(self.product_done, 1)


def segment_sum(nc, z, name, table, keyF, out, gather, scale=None, extras=None, extras_out=None):
    source, index = gather
    with ExitStack() as ctx:
        m = Mem(nc, ctx, name)
        data = m.sb("rows", [P, 2, S, C if extras is None else C + 2])
        scaled = m.sb("rows_scaled", [P, 2, S, C]) if scale is not None else data
        stage = m.sb("index_stage", [P, 2, S], I32)
        landed = [m.sem(f"landed{q}") for q in range(2)]
        staged, waited, scaled_ready, cleared = (m.sem(s) for s in ("staged", "waited", "scaled_ready", "cleared"))
        scatter = Scatter(nc, z, m, table, keyF, out, extras_out)

        with nc.Block() as block:
            @block.gpsimd
            def _(pool):
                pool.memset(out[:], 0.0).then_inc(cleared, 1)
                if extras is not None:
                    pool.memset(extras_out[:], 0.0).then_inc(cleared, 1)

                def gathers(g, q):
                    pool.wait_ge(staged, g + 1)
                    pool.sem_inc(waited, 1)
                    for j in range(S):
                        pool.indirect_dma_start(data[:, q, j, 0:C], None, source,
                                                bass.IndirectOffsetOnAxis(ap=stage[:, q, j:j + 1], axis=0),
                                                ).then_inc(landed[q], 16)
                pairs(z, pool, gathers, z.NS)

            @block.scalar
            def _(act):
                def indices(g, q):
                    if not peeled(g):
                        if scale is None:
                            act.wait_ge(scatter.unit_done, 2 * g)
                        else:
                            act.wait_ge(scaled_ready, g * S - S)
                    if extras is not None:
                        act.activation(data[:, q, :, C:C + 2], extras[:, bass.ds(g * S, S), :], ACT.Copy)
                    act.activation(stage[:, q, :], index[:, bass.ds(g * S, S)], ACT.Copy).then_inc(staged, 1)

                def scaling(g, q):
                    act.wait_ge(landed[q], parity_count(g, q) * S)
                    if not peeled(g):
                        act.wait_ge(scatter.unit_done, 2 * g)
                    for j in range(S):
                        act.activation(scaled[:, q, j, :], data[:, q, j, :], ACT.Copy,
                                       scale=scale[:, bass.ds(g * S + j, 1)]).then_inc(scaled_ready, 1)
                if scale is None:
                    pairs(z, act, indices, z.NS)
                else:
                    indices(0, 0)
                    indices(1, 1)
                    scaling(0, 0)
                    with act.Fori(1, z.NS // 2) as i:
                        indices(2 * i, 0)
                        scaling(2 * i - 1, 1)
                        indices(2 * i + 1, 1)
                        scaling(2 * i, 0)
                    scaling(z.NS - 1, 1)

            @block.vector
            def _(dve):
                dve.wait_ge(cleared, 1 if extras is None else 2)
                scatter.start_vector(dve)
                pairs(z, dve, lambda g, q: scatter.vector(dve, g * S, g * 4), z.NS)
                scatter.finish_vector(dve)

            @block.tensor
            def _(pe):
                scatter.start_tensor(pe)

                def products(g, q):
                    def wait_row(j):
                        if scale is not None:
                            pe.wait_ge(scaled_ready, g * S + (j + 1))
                        elif j == 0:
                            pe.wait_ge(landed[q], parity_count(g, q) * S)
                    scatter.tensor(pe, g * S, g * 4, lambda j: scaled[:, q, j, :], wait_row)
                pairs(z, pe, products, z.NS)



def norm_relu(dve, link, act_var, act_std, seq, x, out, b):
    dve.sem_inc(b.waited, 1)
    link(dve.tensor_reduce(b.mean[:], x, AX_X, ALU.add))
    link(dve.tensor_scalar(b.mean[:], b.mean[:], -1.0 / C, None, ALU.mult))
    link(dve.tensor_tensor(b.cent[:], x, bcast(b.mean[:], C), ALU.add))
    link(dve.tensor_tensor(b.sq[:], b.cent[:], b.cent[:], ALU.mult))
    dve.tensor_reduce(b.var[:], b.sq[:], AX_X, ALU.add).then_inc(act_var, 1)
    dve.wait_ge(act_std, seq)
    link(dve.reciprocal(b.rstd[:], b.std[:]))
    link(dve.tensor_tensor(b.sq[:], b.cent[:], bcast(b.rstd[:], C), ALU.mult))
    link(dve.tensor_scalar(out, b.sq[:], 0.0, None, ALU.max))


class NormBuffers:
    LINKS = 7

    def __init__(self, m):
        self.waited = m.sem("waited")
        self.mean = m.sb("n_mean", [P, B7])
        self.cent = m.sb("n_cent", [P, B7, C])
        self.sq = m.sb("n_sq", [P, B7, C])
        self.var = m.sb("n_var", [P, B7])
        self.std = m.sb("n_std", [P, B7])
        self.rstd = m.sb("n_rstd", [P, B7])


def act_root(act, z, b, act_var, act_std, seq):
    act.wait_ge(act_var, seq)
    act.activation(b.std[:], b.var[:], ACT.Sqrt, bias=z.eps[:], scale=1.0 / C).then_inc(act_std, 1)


def entry(nc, z, x, tabA, tabB, w1, b1):
    A = z.A
    steps = A // B7
    with ExitStack() as ctx:
        m = Mem(nc, ctx, "entry")
        b = NormBuffers(m)
        h = m.sb("h", [P, B7, C])
        hT = m.sb("hT", [P, B7, P])
        w = m.sb("w_ab", [P, 2, C])
        wc = m.sb("w_ab_centred", [P, 2, C])
        wm = m.sb("w_ab_mean", [P, 2])
        bias = m.sb("bias_ab", [1, 2, C])
        brow = m.sb("b1_row", [1, C])
        bm = m.sb("b1_mean", [1, 1])
        ab = m.sb("ab", [P, A, 2 * C])
        psT = m.psum("psT", [P, 8, P])
        psM = m.psum("psM", [P, 8, 2 * C])
        x_in, x_pad, w_in, links = m.sem("x_in"), m.sem("x_pad"), m.sem("w_in"), m.sem("links")
        var_ready, std_ready, h_ready = m.sem("var_ready"), m.sem("std_ready"), m.sem("h_ready")
        t_ready, hT_ready, m_ready, w_ready = m.sem("t_ready"), m.sem("hT_ready"), m.sem("m_ready"), m.sem("w_ready")
        ab_ready, ab_out = m.sem("ab_ready"), m.sem("ab_out")
        fullt = z.N // P
        rest = z.N - fullt * P
        L = NormBuffers.LINKS + 1
        with nc.Block() as block:
            @block.gpsimd
            def _(pool):
                pool.memset(z.X[:, A - 1, :], 0.0).then_inc(x_pad, 1)

            @block.sync
            def _(sp):
                sp.dma_start(z.X[:, 0:fullt, :], x[0:fullt * P, :].rearrange("(a p) f -> p a f", p=P)
                             ).then_inc(x_in, 16)
                sp.dma_start(w[:], w1.rearrange("(h k) f -> k h f", h=2)).then_inc(w_in, 16)
                sp.dma_start(brow[:], b1.rearrange("(o f) -> o f", o=1)).then_inc(w_in, 16)
                sp.wait_ge(x_pad, 1)
                sp.dma_start(z.X[0:rest, fullt, :], x[fullt * P:z.N, :]).then_inc(x_in, 16)
                sp.wait_ge(ab_ready, steps)
                sp.dma_start(node_rows(tabA, 0, A), ab[:, :, 0:C]).then_inc(ab_out, 16)
                sp.dma_start(node_rows(tabB, 0, A), ab[:, :, C:2 * C]).then_inc(ab_out, 16)
                sp.wait_ge(ab_out, 32)

            @block.vector
            def _(dve):
                pre = Link(dve, links)
                dve.wait_ge(w_in, 32)
                pre(dve.tensor_reduce(wm[:], w[:], AX_X, ALU.add))
                pre(dve.tensor_scalar(wm[:], wm[:], -1.0 / C, None, ALU.mult))
                pre(dve.tensor_tensor(wc[:], w[:], bcast(wm[:], C), ALU.add))
                pre(dve.memset(bias[:], 0.0))
                pre(dve.tensor_reduce(bm[:], brow[:], AX_X, ALU.add))
                pre(dve.tensor_scalar(bm[:], bm[:], -1.0 / C, None, ALU.mult))
                dve.tensor_scalar(bias[:, 1, :], brow[:], bm[:, 0:1], None, ALU.add).then_inc(w_ready, 1)
                dve.wait_ge(x_in, 32)
                with dve.Fori(0, steps) as i:
                    link = Link(dve, links, pre.n + i * L)
                    norm_relu(dve, link, var_ready, std_ready, i + 1, z.X[:, bass.ds(i * B7, B7), :], h[:], b)
                    dve.sem_inc(h_ready, 1)
                    dve.wait_ge(m_ready, i + 1)
                    link(dve.tensor_copy(ab[:, bass.ds(i * B7, B7), :], psM[:, 0:B7, :]))
                    dve.sem_inc(ab_ready, 1)

            @block.scalar
            def _(act):
                with act.Fori(0, steps) as i:
                    act_root(act, z, b, var_ready, std_ready, i + 1)
                    act.wait_ge(t_ready, i + 1)
                    act.activation(hT[:], psT[:, 0:B7, :], ACT.Copy).then_inc(hT_ready, 1)

            @block.tensor
            def _(pe):
                pe.wait_ge(w_ready, 1)
                with pe.Fori(0, steps) as i:
                    pe.wait_ge(h_ready, i + 1)
                    for j in range(B7):
                        ins = pe.transpose(psT[:, j, :], h[:, j, :], z.ident[:])
                    ins.then_inc(t_ready, 1)
                    pe.wait_ge(hT_ready, i + 1)
                    for j in range(B7):
                        pe.matmul(psM[:, j, :], z.ones[0:1, :], bias[:].rearrange("o h f -> o (h f)"),
                                  start=True, stop=False)
                        ins = pe.matmul(psM[:, j, :], hT[:, j, :], wc[:].rearrange("k h f -> k (h f)"),
                                        start=False, stop=True)
                    ins.then_inc(m_ready, 1)


def edge_mlp(nc, z, tabA, tabB, table, w2, b2, g1, be1, g2, be2):
    NG = z.NG
    with ExitStack() as ctx:
        m = Mem(nc, ctx, "mlp")
        ga = m.sb("ga", [P, 2, G, C])
        gb = m.sb("gb", [P, 2, G, C])
        stage = m.sb("index_stage", [P, 2, 2, G], I32)
        staged, waited = m.sem("staged"), m.sem("waited")
        u = m.sb("u", [P, 2, G, C])
        y = m.sb("y", [P, 2, G, C])
        vT = m.sb("vT", [P, 2, G, P])
        zT = m.sb("zT", [P, 2, G, P])
        y2 = m.sb("y2", [P, 2, G, C])
        y3 = m.sb("y3", [P, 2, G, C])
        out = m.sb("msg", [P, 2, G, C])
        weighted = m.sb("msg_weighted", [P, 4, G, C])
        junk = m.sb("squares", [P, 2, 2, G, C])
        var = m.sb("var", [P, 2, 2, G])
        std = m.sb("std", [P, 2, 2, G])
        rstd = m.sb("rstd", [P, 2, 2, G])
        cols = m.sb("cols", [P, 2])
        rowsb = m.sb("rowsb", [P, 2, C])
        w = m.sb("w2", [P, C])
        wc = m.sb("w2_centred", [P, C])
        wm = m.sb("w2_mean", [P, 1])
        brow = m.sb("b2_row", [1, C])
        bias = m.sb("b2_centred", [1, C])
        bm = m.sb("b2_mean", [1, 1])
        psT = m.psum("psT", [P, 2, G * P])
        psH = m.psum("psH", [P, 2, G, P])
        gathered = [m.sem(f"gathered{q}") for q in range(2)]
        w_in, w_ready, links = m.sem("w_in"), m.sem("w_ready"), m.sem("links")
        u_ready, var1, std1, r1, y_ready = (m.sem(s) for s in ("u_ready", "var1_ready", "std1_ready", "r1_ready", "y_ready"))
        t_ready, z_ready, h_ready = m.sem("t_ready"), m.sem("z_ready"), m.sem("h_ready")
        v_ready = m.sem("v_ready")
        var2, std2, r2, y2_ready, y3_ready = (m.sem(s) for s in ("var2_ready", "std2_ready", "r2_ready", "y2_ready", "y3_ready"))
        weighted_each = m.sem("weighted_each")
        out_ready, weighted_ready, cleared = m.sem("out_ready"), m.sem("weighted_ready"), m.sem("cleared")
        scatter = Scatter(nc, z, m, table, z.dstF, z.SUM)

        def skewed(eng, *stages):
            deepest = max(lag for _, lag in stages)
            ahead = max(0, -min(lag for _, lag in stages))
            assert ahead % 2 == 0
            lead = deepest + 2 + deepest % 2

            def step(k, parity):
                for body, lag in stages:
                    if not isinstance(k, int) or 0 <= k - lag < NG:
                        body(k - lag, (parity + lag) % 2)
            for k in range(lead):
                step(k, k % 2)
            with eng.Fori(lead // 2, (NG - ahead) // 2) as i:
                step(2 * i, 0)
                step(2 * i + 1, 1)
            for k in range(NG - ahead, NG + deepest):
                step(k, k % 2)

        with nc.Block() as block:
            @block.gpsimd
            def _(pool):
                pool.memset(z.SUM[:], 0.0).then_inc(cleared, 1)

                def gathers(g, q):
                    pool.wait_ge(staged, g + 1)
                    pool.sem_inc(waited, 1)
                    for j in range(G):
                        for side, rows_of, rows in ((0, tabA, ga), (1, tabB, gb)):
                            pool.indirect_dma_start(
                                rows[:, q, j, :], None, rows_of,
                                bass.IndirectOffsetOnAxis(ap=stage[:, q, side, j:j + 1], axis=0),
                            ).then_inc(gathered[q], 16)
                pairs(z, pool, gathers)

            @block.sync
            def _(sp):
                sp.dma_start(w[:], w2).then_inc(w_in, 16)
                sp.dma_start(brow[:], b2.rearrange("(o f) -> o f", o=1)).then_inc(w_in, 16)
                sp.dma_start(cols[:, 0:1], g1.rearrange("(f o) -> f o", o=1)).then_inc(w_in, 16)
                sp.dma_start(cols[:, 1:2], be1.rearrange("(f o) -> f o", o=1)).then_inc(w_in, 16)
                sp.dma_start(rowsb[:, 0, :], g2.partition_broadcast(P)).then_inc(w_in, 16)
                sp.dma_start(rowsb[:, 1, :], be2.partition_broadcast(P)).then_inc(w_in, 16)

            @block.vector
            def _(dve):
                pre = Link(dve, links)
                dve.wait_ge(w_in, 6 * 16)
                pre(dve.tensor_reduce(wm[:], w[:], AX_X, ALU.add))
                pre(dve.tensor_scalar(wm[:], wm[:], -1.0 / C, None, ALU.mult))
                dve.tensor_scalar(wc[:], w[:], wm[:, 0:1], None, ALU.add).then_inc(w_ready, 1)
                pre(dve.tensor_reduce(bm[:], brow[:], AX_X, ALU.add))
                pre(dve.tensor_scalar(bm[:], bm[:], -1.0 / C, None, ALU.mult))
                dve.tensor_scalar(bias[:], brow[:], bm[:, 0:1], None, ALU.add).then_inc(w_ready, 1)

                def add(g, q):
                    dve.wait_ge(gathered[q], parity_count(g, q) * (2 * G))
                    if not peeled(g):
                        dve.wait_ge(y_ready, g - 1)
                        dve.wait_ge(var1, g - 1)
                    dve.tensor_tensor(u[:, q, :, :], ga[:, q, :, :], gb[:, q, :, :], ALU.add).then_inc(u_ready, 1)

                def scale(g, q):
                    dve.wait_ge(std1, g + 1)
                    dve.reciprocal(rstd[:, q, 0, :], std[:, q, 0, :]).then_inc(r1, 1)
                    dve.wait_ge(r1, g + 1)
                    if not peeled(g):
                        dve.wait_ge(t_ready, g - 1)
                    for j in range(G):
                        ins = dve.tensor_scalar(y[:, q, j, :], u[:, q, j, :], rstd[:, q, 0, j:j + 1], None, ALU.mult)
                    ins.then_inc(y_ready, 1)

                def leaky1(g, q):
                    dve.wait_ge(v_ready, g + 1)
                    if not peeled(g):
                        dve.wait_ge(h_ready, g - 1)
                    dve.scalar_tensor_tensor(out=zT[:, q, :, :], in0=vT[:, q, :, :], scalar=SLOPE, in1=vT[:, q, :, :],
                                             op0=ALU.mult, op1=ALU.max).then_inc(z_ready, 1)

                def layer2(g, q):
                    dve.wait_ge(std2, g + 1)
                    dve.reciprocal(rstd[:, q, 1, :], std[:, q, 1, :]).then_inc(r2, 1)
                    dve.wait_ge(r2, g + 1)
                    for j in range(G):
                        ins = dve.scalar_tensor_tensor(out=y2[:, q, j, :], in0=psH[:, q, j, :],
                                                       scalar=rstd[:, q, 1, j:j + 1], in1=rowsb[:, 0, :],
                                                       op0=ALU.mult, op1=ALU.mult)
                    ins.then_inc(y2_ready, 1)
                    dve.wait_ge(y2_ready, g + 1)
                    dve.tensor_tensor(y3[:, q, :, :], y2[:, q, :, :], bcast_mid(rowsb[:, 1, :], G), ALU.add
                                      ).then_inc(y3_ready, 1)
                    dve.wait_ge(y3_ready, g + 1)
                    if not peeled(g):
                        dve.wait_ge(weighted_ready, g - 1)
                    dve.scalar_tensor_tensor(out=out[:, q, :, :], in0=y3[:, q, :, :], scalar=SLOPE,
                                             in1=y3[:, q, :, :], op0=ALU.mult, op1=ALU.max).then_inc(out_ready, 1)

                def one_hots(g, q):
                    if q == 1:
                        scatter.vector(dve, (g - 1) * G, (g - 1) * 2)

                dve.wait_ge(cleared, 1)
                scatter.start_vector(dve)
                skewed(dve, (scale, 1), (add, 0), (layer2, 3), (leaky1, 1), (one_hots, 4))
                scatter.finish_vector(dve)

            @block.scalar
            def _(act):
                def indices(g, q):
                    if not peeled(g):
                        act.wait_ge(u_ready, g - 1)
                    act.activation(stage[:, q, 0, :], z.srcI[:, bass.ds(g * G, G)], ACT.Copy)
                    act.activation(stage[:, q, 1, :], z.dstI[:, bass.ds(g * G, G)], ACT.Copy).then_inc(staged, 1)

                def root(g, q, layer, squares, var_sem, std_sem, used):
                    for j in range(G):
                        ins = act.activation(junk[:, q, layer, j, :], squares[:, q, j, :], ACT.Square,
                                             accum_out=var[:, q, layer, j:j + 1])
                    ins.then_inc(var_sem, 1)
                    act.wait_ge(var_sem, g + 1)
                    if not peeled(g):
                        act.wait_ge(used, g - 1)
                    act.activation(std[:, q, layer, :], var[:, q, layer, :], ACT.Sqrt, bias=z.eps[:], scale=1.0 / C
                                   ).then_inc(std_sem, 1)

                def root1(g, q):
                    act.wait_ge(u_ready, g + 1)
                    root(g, q, 0, u, var1, std1, r1)

                def root2(g, q):
                    act.wait_ge(h_ready, g + 1)
                    root(g, q, 1, psH, var2, std2, r2)

                def affine1(g, q):
                    act.wait_ge(t_ready, g + 1)
                    if not peeled(g):
                        act.wait_ge(z_ready, g - 1)
                    act.activation(vT[:, q, :, :], psT[:, q, :].rearrange("p (j e) -> p j e", j=G), ACT.Identity,
                                   bias=cols[:, 1:2], scale=cols[:, 0:1]).then_inc(v_ready, 1)

                def weigh(g, q):
                    act.wait_ge(out_ready, g + 1)
                    if q == 0 and not (isinstance(g, int) and g < 4):
                        act.wait_ge(scatter.unit_done, g)
                    for j in range(G):
                        act.activation(weighted[:, bass.ds(g % 4, 1), j, :], out[:, q, j, :], ACT.Copy,
                                       scale=z.one_w[:, bass.ds(g * G + j, 1), 1]).then_inc(weighted_each, 1)
                    act.wait_ge(weighted_each, g * G + G)
                    act.sem_inc(weighted_ready, 1)

                act.wait_ge(w_in, 6 * 16)
                indices(0, 0)
                indices(1, 1)
                skewed(act, (affine1, 1), (indices, -2), (root1, 0), (weigh, 3), (root2, 1))

            @block.tensor
            def _(pe):
                def turn(g, q):
                    pe.wait_ge(y_ready, g + 1)
                    if not peeled(g):
                        pe.wait_ge(v_ready, g - 1)
                    for j in range(G):
                        ins = pe.transpose(psT[:, q, j * P:(j + 1) * P], y[:, q, j, :], z.ident[:])
                    ins.then_inc(t_ready, 1)

                def layer2(g, q):
                    pe.wait_ge(z_ready, g + 1)
                    if not peeled(g):
                        pe.wait_ge(y2_ready, g - 1)
                        pe.wait_ge(var2, g - 1)
                    for j in range(G):
                        pe.matmul(psH[:, q, j, :], z.ones[0:1, :], bias[:], start=True, stop=False)
                        ins = pe.matmul(psH[:, q, j, :], zT[:, q, j, :], wc[:], start=False, stop=True)
                    ins.then_inc(h_ready, 1)

                def sums(g, q):
                    if q == 1:
                        first = (g - 1) * G
                        scatter.tensor(pe, first, (g - 1) * 2,
                                       lambda j: weighted[:, bass.ds((g - 1 + j // G) % 4, 1), j % G, :],
                                       lambda j: pe.wait_ge(weighted_each, first + (j + 1)))
                pe.wait_ge(w_ready, 2)
                scatter.start_tensor(pe)
                skewed(pe, (turn, 1), (layer2, 1), (sums, 4))


def after_mlp(nc, z, tabH):
    A = z.A
    steps = A // B7
    with ExitStack() as ctx:
        m = Mem(nc, ctx, "after_mlp")
        b = NormBuffers(m)
        links, var_ready, std_ready = m.sem("links"), m.sem("var_ready"), m.sem("std_ready")
        h_ready, h_out = m.sem("h_ready"), m.sem("h_out")
        L = NormBuffers.LINKS + 1
        with nc.Block() as block:
            @block.sync
            def _(sp):
                sp.wait_ge(h_ready, steps)
                sp.dma_start(node_rows(tabH, 0, A), z.H[:]).then_inc(h_out, 16)
                sp.wait_ge(h_out, 16)

            @block.vector
            def _(dve):
                with dve.Fori(0, steps) as i:
                    link = Link(dve, links, i * L)
                    xs = z.X[:, bass.ds(i * B7, B7), :]
                    link(dve.tensor_tensor(xs, xs, z.SUM[:, bass.ds(i * B7, B7), :], ALU.add))
                    norm_relu(dve, link, var_ready, std_ready, i + 1, xs, z.H[:, bass.ds(i * B7, B7), :], b)
                    dve.sem_inc(h_ready, 1)

            @block.scalar
            def _(act):
                with act.Fori(0, steps) as i:
                    act_root(act, z, b, var_ready, std_ready, i + 1)


def sage_layer(nc, z, name, w_l, b_l, w_r, hidden_table=None, attention=None):
    A = z.A
    steps = A // B7
    D = 4 + 4 + C
    with ExitStack() as ctx:
        m = Mem(nc, ctx, name)
        mean = m.sb("mean", [P, B7, C])
        hs = m.sb("hs", [P, B7, C])
        turned = m.sb("turned", [P, 2 * B7, P])
        wl, wr, brow = m.sb("wl", [P, C]), m.sb("wr", [P, C]), m.sb("brow", [1, C])
        psT = m.psum("psT", [P, 4 * 4, P])
        psM = m.psum("psM", [P, 8, 2 * C])
        w_in, links, raw_set = m.sem("w_in"), m.sem("links"), m.sem("raw_set")
        bias_set = m.sem("bias_set")
        in_ready, t_ready, turned_ready, m_ready = (m.sem(s) for s in ("in_ready", "t_ready", "turned_ready", "m_ready"))
        var_ready, std_ready = m.sem("var_ready"), m.sem("std_ready")
        t2_ready, turned2_ready, m2_ready = m.sem("t2_ready"), m.sem("turned2_ready"), m.sem("m2_ready")
        h3_ready, tabs_ready, tabs_out = m.sem("h3_ready"), m.sem("tabs_ready"), m.sem("tabs_out")
        weights_turned, weights_ready = m.sem("weights_turned"), m.sem("weights_ready")
        last = attention is not None
        if last:
            wq, wk, wo, bo, tabQ, tabK, tabV = attention
            b = NormBuffers(m)
            h3 = m.sb("h3", [P, B7, C])
            raw = m.sb("raw", [P, 2, P])
            wcat = m.sb("wcat", [P, D])
            bcat = m.sb("bcat", [1, D])
            qk = m.sb("qk", [P, A, 8])
            qk0 = m.sb("qk0", [P, B7, 4])
            hv = m.sb("hv", [P, A, C])
            L = 3 + 1 + NormBuffers.LINKS + 4
        else:
            L = 3 + 1
        PRE = 0 if last else 2

        with nc.Block() as block:
            @block.sync
            def _(sp):
                sp.dma_start(wl[:], w_l).then_inc(w_in, 16)
                sp.dma_start(wr[:], w_r).then_inc(w_in, 16)
                sp.dma_start(brow[:], b_l.rearrange("(o f) -> o f", o=1)).then_inc(w_in, 16)
                if last:
                    sp.wait_ge(raw_set, 1)
                    sp.wait_ge(bias_set, 1)
                    sp.dma_start(raw[0:4, 0, :], wq).then_inc(w_in, 16)
                    sp.dma_start(raw[4:8, 0, :], wk).then_inc(w_in, 16)
                    sp.dma_start(raw[:, 1, :], wo).then_inc(w_in, 16)
                    sp.dma_start(bcat[:, 8:D], bo.rearrange("(o f) -> o f", o=1)).then_inc(w_in, 16)
                sp.wait_ge(tabs_ready, steps)
                if last:
                    sp.dma_start(node_rows(tabQ, 0, A), qk[:, :, 0:4]).then_inc(tabs_out, 16)
                    sp.dma_start(node_rows(tabK, 0, A), qk[:, :, 4:8]).then_inc(tabs_out, 16)
                    sp.dma_start(node_rows(tabV, 0, A), hv[:]).then_inc(tabs_out, 16)
                    sp.wait_ge(tabs_out, 48)
                else:
                    sp.dma_start(node_rows(hidden_table, 0, A), z.H[:]).then_inc(tabs_out, 16)
                    sp.wait_ge(tabs_out, 16)

            @block.vector
            def _(dve):
                if last:
                    dve.memset(bcat[:], 0.0).then_inc(bias_set, 1)
                    dve.wait_ge(weights_turned, 1)
                    dve.tensor_copy(wcat[:, 0:8], psT[:, 0, 0:8]).then_inc(weights_ready, 1)
                    dve.tensor_copy(wcat[:, 8:D], psT[:, 1, :]).then_inc(weights_ready, 1)
                else:
                    pre = Link(dve, links)
                    pre(dve.tensor_scalar(z.rcount[:], z.SUMX[:, :, 0], 1.0, None, ALU.max))
                    pre(dve.reciprocal(z.rcount[:], z.rcount[:]))
                with dve.Fori(0, steps) as i:
                    link = Link(dve, links, PRE + i * L)
                    tiles = bass.ds(i * B7, B7)
                    link(dve.tensor_tensor(mean[:], z.SUM[:, tiles, :], bcast(z.rcount[:, tiles], C), ALU.mult))
                    link(dve.tensor_copy(hs[:], z.H[:, tiles, :]))
                    dve.sem_inc(in_ready, 1)
                    dve.wait_ge(m_ready, i + 1)
                    if not last:
                        link(dve.tensor_scalar(z.H[:, tiles, :], psM[:, 0:B7, 0:C], 0.0, None, ALU.max))
                        link(dve.memset(mean[:, 0, 0:1], 0.0))
                        dve.sem_inc(tabs_ready, 1)
                    else:
                        link(dve.tensor_tensor(z.X[:, tiles, :], z.X[:, tiles, :], psM[:, 0:B7, 0:C], ALU.add))
                        norm_relu(dve, link, var_ready, std_ready, i + 1, z.X[:, tiles, :], h3[:], b)
                        dve.sem_inc(h3_ready, 1)
                        dve.wait_ge(m2_ready, i + 1)
                        link(dve.tensor_copy(hv[:, tiles, :], psM[:, 0:B7, 8:D]))
                        link(dve.tensor_copy(qk[:, tiles, 0:4], psM[:, 0:B7, 0:4]))
                        link(dve.tensor_scalar(qk0[:], psM[:, 0:B7, 4:8], SLOPE, None, ALU.mult))
                        link(dve.tensor_tensor(qk[:, tiles, 4:8], psM[:, 0:B7, 4:8], qk0[:], ALU.max))
                        link(dve.memset(mean[:, 0, 0:1], 0.0))
                        dve.sem_inc(tabs_ready, 1)

            @block.scalar
            def _(act):
                with act.Fori(0, steps) as i:
                    act.wait_ge(t_ready, i + 1)
                    act.activation(turned[:], psT[:, 0:2 * B7, :], ACT.Copy).then_inc(turned_ready, 1)
                    if last:
                        act_root(act, z, b, var_ready, std_ready, i + 1)
                        act.wait_ge(t2_ready, i + 1)
                        act.activation(turned[:, 0:B7, :], psT[:, 0:B7, :], ACT.Copy).then_inc(turned2_ready, 1)

            @block.gpsimd
            def _(pool):
                if last:
                    pool.memset(raw[:, 0, :], 0.0).then_inc(raw_set, 1)

            @block.tensor
            def _(pe):
                pe.wait_ge(w_in, (7 if last else 3) * 16)
                if last:
                    pe.transpose(psT[:, 0, :], raw[:, 0, :], z.ident[:])
                    pe.transpose(psT[:, 1, :], raw[:, 1, :], z.ident[:]).then_inc(weights_turned, 1)
                    pe.wait_ge(weights_ready, 2)
                with pe.Fori(0, steps) as i:
                    pe.wait_ge(in_ready, i + 1)
                    for j in range(B7):
                        pe.transpose(psT[:, 2 * j, :], mean[:, j, :], z.ident[:])
                        ins = pe.transpose(psT[:, 2 * j + 1, :], hs[:, j, :], z.ident[:])
                    ins.then_inc(t_ready, 1)
                    pe.wait_ge(turned_ready, i + 1)
                    for j in range(B7):
                        pe.matmul(psM[:, j, 0:C], z.ones[0:1, :], brow[:], start=True, stop=False)
                        pe.matmul(psM[:, j, 0:C], turned[:, 2 * j, :], wl[:], start=False, stop=False)
                        ins = pe.matmul(psM[:, j, 0:C], turned[:, 2 * j + 1, :], wr[:], start=False, stop=True)
                    ins.then_inc(m_ready, 1)
                    if last:
                        pe.wait_ge(h3_ready, i + 1)
                        for j in range(B7):
                            ins = pe.transpose(psT[:, j, :], h3[:, j, :], z.ident[:])
                        ins.then_inc(t2_ready, 1)
                        pe.wait_ge(turned2_ready, i + 1)
                        for j in range(B7):
                            pe.matmul(psM[:, j, 0:D], z.ones[0:1, :], bcat[:], start=True, stop=False)
                            ins = pe.matmul(psM[:, j, 0:D], turned[:, j, :], wcat[:], start=False, stop=True)
                        ins.then_inc(m2_ready, 1)


def after_attention(nc, z, tabX, w):
    A = z.A
    steps = A // B7
    with ExitStack() as ctx:
        m = Mem(nc, ctx, "after_attention")
        b = NormBuffers(m)
        act7 = m.sb("leaky", [P, B7, C])
        h = m.sb("h", [P, B7, C])
        hT = m.sb("hT", [P, B7, P])
        ws = m.sb("w", [P, C])
        degree, above, root = m.sb("degree", [P, A]), m.sb("above", [P, A]), m.sb("root", [P, A])
        psT = m.psum("psT", [P, 8, P])
        psM = m.psum("psM", [P, 8, C])
        names = ("w_in", "links", "degree_ready", "root_ready", "var_ready", "std_ready", "h_ready", "t_ready",
                 "hT_ready", "m_ready", "tab_ready", "tab_out")
        (w_in, links, degree_ready, root_ready, var_ready, std_ready, h_ready, t_ready, hT_ready, m_ready, tab_ready,
         tab_out) = (m.sem(s) for s in names)
        L = 2 + NormBuffers.LINKS + 1
        with nc.Block() as block:
            @block.sync
            def _(sp):
                sp.dma_start(ws[:], w).then_inc(w_in, 16)
                sp.wait_ge(tab_ready, steps)
                sp.dma_start(node_rows(tabX, 0, A), z.H[:]).then_inc(tab_out, 16)
                sp.wait_ge(tab_out, 16)

            @block.vector
            def _(dve):
                pre = Link(dve, links)
                pre(dve.tensor_scalar(degree[:], z.SUMX[:, :, 1], 1.0, None, ALU.add))
                pre(dve.tensor_scalar(above[:], degree[:], 0.0, None, ALU.is_gt))
                dve.tensor_scalar(degree[:], degree[:], 1e-30, None, ALU.max).then_inc(degree_ready, 1)
                dve.wait_ge(root_ready, 1)
                pre(dve.reciprocal(degree[:], root[:]))
                pre(dve.tensor_tensor(z.dinv[:], degree[:], above[:], ALU.mult))
                with dve.Fori(0, steps) as i:
                    link = Link(dve, links, pre.n + i * L)
                    tiles = bass.ds(i * B7, B7)
                    link(dve.scalar_tensor_tensor(out=act7[:], in0=z.SUM[:, tiles, :], scalar=SLOPE,
                                                  in1=z.SUM[:, tiles, :], op0=ALU.mult, op1=ALU.max))
                    link(dve.tensor_tensor(z.X[:, tiles, :], z.X[:, tiles, :], act7[:], ALU.add))
                    norm_relu(dve, link, var_ready, std_ready, i + 1, z.X[:, tiles, :], h[:], b)
                    dve.sem_inc(h_ready, 1)
                    dve.wait_ge(m_ready, i + 1)
                    link(dve.tensor_tensor(z.H[:, tiles, :], psM[:, 0:B7, :], bcast(z.dinv[:, tiles], C), ALU.mult))
                    dve.sem_inc(tab_ready, 1)

            @block.scalar
            def _(act):
                act.wait_ge(degree_ready, 1)
                act.activation(root[:], degree[:], ACT.Sqrt).then_inc(root_ready, 1)
                with act.Fori(0, steps) as i:
                    act_root(act, z, b, var_ready, std_ready, i + 1)
                    act.wait_ge(t_ready, i + 1)
                    act.activation(hT[:], psT[:, 0:B7, :], ACT.Copy).then_inc(hT_ready, 1)

            @block.tensor
            def _(pe):
                pe.wait_ge(w_in, 16)
                with pe.Fori(0, steps) as i:
                    pe.wait_ge(h_ready, i + 1)
                    for j in range(B7):
                        ins = pe.transpose(psT[:, j, :], h[:, j, :], z.ident[:])
                    ins.then_inc(t_ready, 1)
                    pe.wait_ge(hT_ready, i + 1)
                    for j in range(B7):
                        ins = pe.matmul(psM[:, j, :], hT[:, j, :], ws[:], start=True, stop=True)
                    ins.then_inc(m_ready, 1)


def finish(nc, z, out, bias):
    A = z.A
    steps = A // B7
    with ExitStack() as ctx:
        m = Mem(nc, ctx, "finish")
        brow = m.sb("bias", [P, C])
        b_in, links, out_ready, out_done = m.sem("b_in"), m.sem("links"), m.sem("out_ready"), m.sem("out_done")
        full = z.N // P
        rest = z.N - full * P
        with nc.Block() as block:
            @block.sync
            def _(sp):
                sp.dma_start(brow[:], bias.partition_broadcast(P)).then_inc(b_in, 16)
                sp.wait_ge(out_ready, 1)
                sp.dma_start(out[0:full * P, :].rearrange("(a p) f -> p a f", p=P), z.X[:, 0:full, :]
                             ).then_inc(out_done, 16)
                sp.dma_start(out[full * P:z.N, :], z.X[0:rest, full, :]).then_inc(out_done, 16)
                sp.wait_ge(out_done, 32)

            @block.vector
            def _(dve):
                link = Link(dve, links)
                dve.wait_ge(b_in, 16)
                link(dve.tensor_tensor(z.SUM[:], z.SUM[:], z.H[:], ALU.add))
                link(dve.tensor_tensor(z.SUM[:], z.SUM[:], bcast(z.dinv[:], C), ALU.mult))
                link(dve.tensor_tensor(z.X[:], z.X[:], bcast_mid(brow[:], A), ALU.add))
                dve.tensor_tensor(z.X[:], z.X[:], z.SUM[:], ALU.add).then_inc(out_ready, 1)




def query_sums(nc, z, tabQ, tabQsum):
    A, NG = z.A, z.NG
    F = 5
    with ExitStack() as ctx:
        m = Mem(nc, ctx, "query_sums")
        key_i, digit_i = m.sb("key_i", [P, z.T], I32), m.sb("digit_i", [P, z.T], I32)
        tiles_row = m.sb("tiles_row", [P, A])
        stage = m.sb("stage", [P, 2, G], I32)
        rows = m.sb("rows", [P, 2, G, F])
        low = m.sb("low_onehot", [P, 2, G, P])
        high = m.sb("high_onehot", [P, 2, G, A])
        prod = m.sb("prod", [P, 2, G, A * F])
        sums = m.sb("sums", [P, A, F])
        below = m.sb("below", [P, P])
        total = m.sb("total", [P, A])
        one_a = m.sb("one_a", [P, A])
        cum = m.sb("cum", [P, A])
        counts = m.sb("counts", [P, A])
        acc = m.psum("acc", [P, A * F])
        ps = m.psum("prefix", [P, 2, A])
        gathered = [m.sem(f"gathered{q}") for q in range(2)]
        consts, links, staged, waited = m.sem("consts"), m.sem("links"), m.sem("staged"), m.sem("waited")
        onehots, prod_ready, used, sums_ready = m.sem("onehots"), m.sem("prod_ready"), m.sem("used"), m.sem("sums_ready")
        acc_ready = m.sem("acc_ready")
        counts_ready, prefix_ready, sums_out = m.sem("counts_ready"), m.sem("prefix_ready"), m.sem("sums_out")

        with nc.Block() as block:
            @block.gpsimd
            def _(pool):
                pool.iota(tiles_row[:], [[1, A]], base=0, channel_multiplier=0,
                          allow_small_or_imprecise_dtypes=True).then_inc(consts, 1)
                pool.memset(rows[:], 1.0).then_inc(consts, 1)
                pool.memset(one_a[:], 1.0).then_inc(consts, 1)
                pool.affine_select(out=below[:], in_=z.ones[:], compare_op=ALU.is_gt, fill=0.0, base=0,
                                   pattern=[[1, P]], channel_multiplier=-1).then_inc(consts, 1)
                pool.wait_ge(consts, 4)

                def gathers(g, q):
                    pool.wait_ge(staged, g + 1)
                    pool.sem_inc(waited, 1)
                    for j in range(G):
                        pool.indirect_dma_start(rows[:, q, j, 0:4], None, tabQ,
                                                bass.IndirectOffsetOnAxis(ap=stage[:, q, j:j + 1], axis=0),
                                                ).then_inc(gathered[q], 16)
                pairs(z, pool, gathers)

            @block.scalar
            def _(act):
                def indices(g, q):
                    if not (isinstance(g, int) and g < 2):
                        act.wait_ge(prod_ready, g - 1)
                    act.activation(stage[:, q, :], z.dstI[:, bass.ds(g * G, G)], ACT.Copy).then_inc(staged, 1)
                pairs(z, act, indices)

            @block.vector
            def _(dve):
                link = Link(dve, links)
                link(dve.tensor_copy(key_i[:], z.srcF[:]))
                link(dve.tensor_scalar(digit_i[:], key_i[:], 7, None, ALU.arith_shift_right))
                link(dve.tensor_copy(z.srcHigh[:], digit_i[:]))
                link(dve.tensor_scalar(key_i[:], key_i[:], P - 1, None, ALU.bitwise_and))
                link(dve.tensor_copy(z.srcLow[:], key_i[:]))
                dve.wait_ge(consts, 4)

                def products(g, q):
                    if not (isinstance(g, int) and g < 2):
                        dve.wait_ge(used, g - 1)
                    cols = bass.ds(g * G, G)
                    dve.tensor_tensor(low[:, q, :, :], bcast(z.srcLow[:, cols], P), bcast_mid(z.iota[:], G),
                                      ALU.is_equal)
                    dve.tensor_tensor(high[:, q, :, :], bcast(z.srcHigh[:, cols], A), bcast_mid(tiles_row[:], G),
                                      ALU.is_equal).then_inc(onehots, 1)
                    dve.wait_ge(onehots, g + 1)
                    dve.wait_ge(gathered[q], (g // 2 + 1) * G * 16 if isinstance(g, int) else (g + (2 - q)) * (G * 8))
                    for j in range(G):
                        ins = dve.tensor_tensor(
                            prod[:, q, j, :].rearrange("p (a f) -> p a f", f=F), bcast(high[:, q, j, :], F),
                            bcast_mid(rows[:, q, j, :], A), ALU.mult)
                    ins.then_inc(prod_ready, 1)
                pairs(z, dve, products)
                dve.wait_ge(acc_ready, 1)
                link(dve.tensor_copy(sums[:], acc[:].rearrange("p (a f) -> p a f", f=F)))
                dve.sem_inc(sums_ready, 1)
                dve.tensor_copy(counts[:], sums[:, :, 4]).then_inc(counts_ready, 1)
                dve.wait_ge(prefix_ready, 1)
                link(dve.tensor_copy(total[:], ps[:, 1, :]))
                link(dve.tensor_tensor_scan(cum[:], one_a[:], total[:], 0.0, ALU.mult, ALU.add))
                link(dve.tensor_tensor(cum[:], cum[:], total[:], ALU.subtract))
                dve.tensor_tensor(z.first[:], cum[:], ps[:, 0, :], ALU.add)

            @block.tensor
            def _(pe):
                pe.matmul(acc[:], z.zero16[:, 0:P], z.zero_wide[:, 0:A * F], start=True, stop=False)

                def products(g, q):
                    pe.wait_ge(prod_ready, g + 1)
                    for j in range(G):
                        ins = pe.matmul(acc[:], low[:, q, j, :], prod[:, q, j, :], start=False, stop=False)
                    ins.then_inc(used, 1)
                pairs(z, pe, products)
                pe.matmul(acc[:], z.zero16[:, 0:P], z.zero_wide[:, 0:A * F], start=False, stop=True
                          ).then_inc(acc_ready, 1)
                pe.wait_ge(counts_ready, 1)
                pe.matmul(ps[:, 0, :], below[:], counts[:], start=True, stop=True)
                pe.matmul(ps[:, 1, :], z.ones[:], counts[:], start=True, stop=True).then_inc(prefix_ready, 1)

            @block.sync
            def _(sp):
                sp.wait_ge(sums_ready, 1)
                sp.dma_start(node_rows(tabQsum, 0, A), sums[:, :, 0:4]).then_inc(sums_out, 16)
                sp.wait_ge(sums_out, 16)


def sort_and_score(nc, z, tabK, tabQsum, sorted_edges):
    A, NG, H = z.A, z.NG, 4
    with ExitStack() as ctx:
        m = Mem(nc, ctx, "sort")
        tiles_row = m.sb("tiles_row", [P, A])
        earlier = m.sb("earlier", [P, P])
        low, lowT = m.sb("low", [P, 2, G, P]), m.sb("lowT", [P, 2, G, P])
        high = m.sb("high", [P, 2, G, A])
        key = m.sb("key", [P, 2, G])
        stage = m.sb("stage", [P, 2, G], I32)
        query = m.sb("query", [P, 2, G, H])
        record = m.sb("record", [P, 2, G, 2 + H])
        lookup = m.sb("lookup", [P, A * (1 + H)])
        running = lookup[:, 0:A]
        key_pick = m.sb("key_pick", [P, 2, G, A, H])
        key_row = m.sb("key_row", [P, 2, G, H])
        picked, same = m.sb("picked", [P, 2, G, A]), m.sb("same", [P, 2, G, P])
        base, within = m.sb("base", [P, 2, G]), m.sb("within", [P, 2, G])
        rank = m.sb("rank", [P, 2, G], I32)
        psT, psK = m.psum("psT", [P, G, P]), m.psum("psK", [P, 2, G, P])
        psG = m.psum("psG", [P, 2, G, 2 * P])
        psR = m.psum("psR", [P, A])
        consts, onehots, turned, keys_turned = m.sem("consts"), m.sem("onehots"), m.sem("turned"), m.sem("keys_turned")
        lowT_ready, counted, running_ready = m.sem("lowT_ready"), m.sem("counted"), m.sem("running_ready")
        sums_ready, rank_ready, waited = m.sem("sums_ready"), m.sem("rank_ready"), m.sem("waited")
        staged, keys_in, key_picked, record_ready = (m.sem(s) for s in ("staged", "keys_in", "key_picked", "record_ready"))
        key_summed, freed = m.sem("key_summed"), m.sem("freed")
        gathered = [m.sem(f"gathered{q}") for q in range(2)]
        scattered = [m.sem(f"scattered{q}") for q in range(2)]

        with nc.Block() as block:
            @block.gpsimd
            def _(pool):
                pool.iota(tiles_row[:], [[1, A]], base=0, channel_multiplier=0,
                          allow_small_or_imprecise_dtypes=True).then_inc(consts, 1)
                pool.affine_select(out=earlier[:], in_=z.ones[:], compare_op=ALU.is_gt, fill=0.0, base=0,
                                   pattern=[[-1, P]], channel_multiplier=1).then_inc(consts, 1)

                def scatter(g, q):
                    pool.wait_ge(record_ready, g + 1)
                    pool.sem_inc(waited, 1)
                    for j in range(G):
                        pool.indirect_dma_start(sorted_edges,
                                                bass.IndirectOffsetOnAxis(ap=rank[:, q, j:j + 1], axis=0),
                                                record[:, q, j, :], None).then_inc(scattered[q], 16)

                def gathers(g, q):
                    pool.wait_ge(staged, g + 1)
                    pool.sem_inc(waited, 1)
                    for j in range(G):
                        pool.indirect_dma_start(query[:, q, j, :], None, tabQsum,
                                                bass.IndirectOffsetOnAxis(ap=stage[:, q, j:j + 1], axis=0),
                                                ).then_inc(gathered[q], 16)
                gathers(0, 0)
                gathers(1, 1)
                scatter(0, 0)
                with pool.Fori(1, NG // 2) as i:
                    gathers(2 * i, 0)
                    scatter(2 * i - 1, 1)
                    gathers(2 * i + 1, 1)
                    scatter(2 * i, 0)
                scatter(NG - 1, 1)
                for q in range(2):
                    pool.wait_ge(scattered[q], NG // 2 * G * 16)

            @block.sync
            def _(sp):
                sp.dma_start(lookup[:, A:A * (1 + H)].rearrange("p (a h) -> p a h", h=H), node_rows(tabK, 0, A)
                             ).then_inc(keys_in, 16)

            @block.vector
            def _(dve):
                dve.wait_ge(consts, 2)

                def one_hots(g, q):
                    if not peeled(g):
                        dve.wait_ge(counted, g * G - G)
                        dve.wait_ge(keys_turned, g - 1)
                    cols = bass.ds(g * G, G)
                    dve.tensor_copy(key[:, q, :], z.srcF[:, cols])
                    dve.tensor_tensor(low[:, q, :, :], bcast(z.srcLow[:, cols], P), bcast_mid(z.iota[:], G),
                                      ALU.is_equal)
                    dve.tensor_tensor(high[:, q, :, :], bcast(z.srcHigh[:, cols], A), bcast_mid(tiles_row[:], G),
                                      ALU.is_equal).then_inc(onehots, 1)

                def ranks(g, q):
                    dve.wait_ge(keys_turned, g + 1)
                    dve.wait_ge(counted, g * G + G)
                    for j in range(G):
                        dve.scalar_tensor_tensor(out=same[:, q, j, :], in0=psK[:, q, j, :], scalar=key[:, q, j:j + 1],
                                                 in1=earlier[:], op0=ALU.is_equal, op1=ALU.mult,
                                                 accum_out=within[:, q, j:j + 1])
                        ins = dve.scalar_tensor_tensor(out=picked[:, q, j, :], in0=psG[:, q, j, 0:A], scalar=1.0,
                                                       in1=high[:, q, j, :], op0=ALU.mult, op1=ALU.mult,
                                                       accum_out=base[:, q, j:j + 1])
                    ins.then_inc(sums_ready, 1)
                    if not peeled(g):
                        dve.wait_ge(scattered[q], (g - q) * (G * 8))
                        dve.sem_inc(freed, 1)
                    dve.tensor_copy(record[:, q, :, 0], z.srcF[:, bass.ds(g * G, G)])
                    dve.tensor_copy(record[:, q, :, 1], z.dstF[:, bass.ds(g * G, G)])
                    dve.wait_ge(sums_ready, g + 1)
                    dve.tensor_tensor(rank[:, q, :], base[:, q, :], within[:, q, :], ALU.add)
                    dve.tensor_tensor(key_pick[:, q, :, :, :],
                                      psG[:, q, :, A:A * (1 + H)].rearrange("p j (a h) -> p j a h", h=H),
                                      high[:, q, :, :].unsqueeze(3).to_broadcast([P, G, A, H]), ALU.mult
                                      ).then_inc(rank_ready, 1)
                    dve.wait_ge(rank_ready, g + 1)
                    dve.tensor_reduce(key_row[:, q, :, :], key_pick[:, q, :, :, :].rearrange("p j a h -> p j h a"),
                                      AX_X, ALU.add).then_inc(key_summed, 1)
                    dve.wait_ge(key_summed, g + 1)
                    dve.wait_ge(gathered[q], parity_count(g, q) * G)
                    dve.tensor_tensor(record[:, q, :, 2:2 + H], key_row[:, q, :, :], query[:, q, :, :], ALU.mult
                                      ).then_inc(record_ready, 1)

                one_hots(0, 0)
                one_hots(1, 1)
                ranks(0, 0)
                with dve.Fori(1, NG // 2) as i:
                    one_hots(2 * i, 0)
                    ranks(2 * i - 1, 1)
                    one_hots(2 * i + 1, 1)
                    ranks(2 * i, 0)
                ranks(NG - 1, 1)

            @block.scalar
            def _(act):
                def turn(g, q):
                    act.wait_ge(turned, g + 1)
                    act.activation(lowT[:, q, :, :], psT[:], ACT.Copy).then_inc(lowT_ready, 1)
                    for j in range(G):
                        act.wait_ge(counted, g * G + (j + 1))
                        act.activation(running, psR[:], ACT.Copy).then_inc(running_ready, 1)
                def indices(g, q):
                    if not peeled(g):
                        act.wait_ge(record_ready, g - 1)
                    act.activation(stage[:, q, :], z.dstI[:, bass.ds(g * G, G)], ACT.Copy).then_inc(staged, 1)

                act.activation(running, z.first[:], ACT.Copy).then_inc(running_ready, 1)
                indices(0, 0)
                indices(1, 1)
                turn(0, 0)
                with act.Fori(1, NG // 2) as i:
                    turn(2 * i - 1, 1)
                    indices(2 * i, 0)
                    turn(2 * i, 0)
                    indices(2 * i + 1, 1)
                turn(NG - 1, 1)

            @block.tensor
            def _(pe):
                def chunk(g, q):
                    pe.wait_ge(onehots, g + 1)
                    if isinstance(g, int) and g < 1:
                        pass
                    else:
                        pe.wait_ge(lowT_ready, g)
                    for j in range(G):
                        ins = pe.transpose(psT[:, j, :], low[:, q, j, :], z.ident[:])
                    ins.then_inc(turned, 1)
                    if not peeled(g):
                        pe.wait_ge(rank_ready, g - 1)
                    for j in range(G):
                        ins = pe.transpose(psK[:, q, j, :], key[:, q, j:j + 1].to_broadcast([P, P]), z.ident[:])
                    ins.then_inc(keys_turned, 1)
                    pe.wait_ge(lowT_ready, g + 1)
                    for j in range(G):
                        pe.wait_ge(running_ready, g * G + (j + 1))
                        pe.matmul(psG[:, q, j, 0:A * (1 + H)], lowT[:, q, j, :], lookup[:], start=True, stop=True)
                        pe.matmul(psR[:], z.ident[:], running, start=True, stop=False)
                        pe.matmul(psR[:], low[:, q, j, :], high[:, q, j, :], start=False, stop=True
                                  ).then_inc(counted, 1)
                pe.wait_ge(keys_in, 16)
                pairs(z, pe, chunk)


def edge_softmax(nc, z, sorted_edges, flat):
    T, H, BIG = z.T, 4, 3.0e38
    with ExitStack() as ctx:
        m = Mem(nc, ctx, "softmax")
        edges = m.sb("edges", [P, T, 2 + H])
        scores = edges[:, :, 2:2 + H]
        powers = m.sb("powers", [P, T, H])
        src, dst = m.sb("src", [P, T]), m.sb("dst", [P, T])
        edges_in = m.sem("edges_in")
        same_prev, same_next = m.sb("same_prev", [P, T]), m.sb("same_next", [P, T])
        pen_prev, pen_next = m.sb("pen_prev", [P, T]), m.sb("pen_next", [P, T])
        fwd, bwd, tmp = m.sb("fwd", [P, T]), m.sb("bwd", [P, T]), m.sb("tmp", [P, T])
        weight = m.sb("weight", [P, T])
        ends = m.sb("ends", [P, 2, H])
        key_rows = m.sb("key_rows", [H, 2, P + 1])
        joined, pen_row = m.sb("joined", [H, 2, P]), m.sb("pen_row", [H, 2, P])
        neighbour = m.sb("neighbour", [P, 2, H])
        col = m.sb("col", [P, H])
        row, chain = m.sb("row", [H, P]), m.sb("chain", [H, P + 1])
        carry = m.sb("carry", [P, H])
        psR, psC = m.psum("psR", [H, 2, P]), m.psum("psC", [P, 2, H])
        psr, psc = m.psum("psr", [H, P]), m.psum("psc", [P, H])
        links, ends_ready, rows_ready, shifted, cols_ready = (m.sem(s) for s in (
            "links", "ends_ready", "rows_ready", "shifted", "cols_ready"))
        col_ready, row_ready, chain_ready, carry_ready = (m.sem(s) for s in (
            "col_ready", "row_ready", "chain_ready", "carry_ready"))
        less_max, powers_ready, weight_ready, flat_out = (m.sem(s) for s in (
            "less_max", "powers_ready", "weight_ready", "flat_out"))
        CHAINS = 4
        with nc.Block() as block:
            @block.vector
            def _(dve):
                link = Link(dve, links)
                dve.wait_ge(edges_in, 16)
                link(dve.tensor_copy(src[:], edges[:, :, 0]))
                link(dve.tensor_copy(dst[:], edges[:, :, 1]))
                for h in range(H):
                    link(dve.tensor_copy(ends[:, 0, h:h + 1], src[:, T - 1:T]))
                    link(dve.tensor_copy(ends[:, 1, h:h + 1], src[:, 0:1]))
                dve.sem_inc(ends_ready, 1)
                link(dve.memset(key_rows[:], -1.0))
                dve.wait_ge(rows_ready, 1)
                link(dve.tensor_copy(key_rows[:, 0, 1:P + 1], psR[:, 0, :]))
                link(dve.tensor_copy(key_rows[:, 1, 0:P], psR[:, 1, :]))
                dve.sem_inc(shifted, 1)
                for d in range(2):
                    link(dve.tensor_tensor(joined[:, d, :], key_rows[:, d, 1:P + 1], key_rows[:, d, 0:P], ALU.is_equal))
                    link(dve.tensor_scalar(pen_row[:, d, :], joined[:, d, :], -1.0, BIG, ALU.add, ALU.mult))
                dve.wait_ge(cols_ready, 1)
                link(dve.tensor_copy(neighbour[:], psC[:]))
                link(dve.tensor_tensor(same_prev[:, 1:T], src[:, 1:T], src[:, 0:T - 1], ALU.is_equal))
                link(dve.tensor_tensor(same_prev[:, 0:1], src[:, 0:1], neighbour[:, 0, 0:1], ALU.is_equal))
                link(dve.tensor_copy(same_next[:, 0:T - 1], same_prev[:, 1:T]))
                link(dve.tensor_tensor(same_next[:, T - 1:T], src[:, T - 1:T], neighbour[:, 1, 0:1], ALU.is_equal))
                link(dve.tensor_scalar(pen_prev[:], same_prev[:], -1.0, BIG, ALU.add, ALU.mult))
                link(dve.tensor_scalar(pen_next[:], same_next[:], -1.0, BIG, ALU.add, ALU.mult))
                used = [0]

                def chained(direction, mask_row, identity, op0, op1):
                    used[0] += 1
                    dve.sem_inc(col_ready, 1)
                    link(dve.memset(chain[:], identity))
                    dve.wait_ge(row_ready, used[0])
                    link(dve.tensor_copy(row[:], psr[:]))
                    if direction == 0:
                        link(dve.tensor_tensor_scan(chain[:, 1:P + 1], mask_row, row[:], identity, op0, op1))
                    else:
                        link(dve.tensor_tensor_scan(chain[:, P - 1::-1], mask_row[:, ::-1], row[:, ::-1], identity,
                                                    op0, op1))
                    dve.sem_inc(chain_ready, 1)
                    dve.wait_ge(carry_ready, used[0])
                    link(dve.tensor_copy(carry[:], psc[:]))

                def forward_max(h, init):
                    link(dve.tensor_tensor_scan(fwd[:], pen_prev[:], scores[:, :, h], init, ALU.add, ALU.max))

                def backward_max(h, init):
                    link(dve.tensor_tensor_scan(bwd[:, ::-1], pen_next[:, ::-1], fwd[:, ::-1], init, ALU.add, ALU.max))

                def forward_sum(h, init):
                    link(dve.tensor_tensor_scan(fwd[:], same_prev[:], powers[:, :, h], init, ALU.mult, ALU.add))

                def backward_sum(h, init):
                    link(dve.tensor_tensor(tmp[:], fwd[:], same_next[:], ALU.mult))
                    link(dve.tensor_tensor(tmp[:], fwd[:], tmp[:], ALU.subtract))
                    link(dve.tensor_tensor_scan(bwd[:, ::-1], same_next[:, ::-1], tmp[:, ::-1], init, ALU.mult, ALU.add))

                carry_f = m.sb("carry_f", [P, 2, H])
                for kind, (forward, backward, ident_f, op0, op1, masks) in enumerate((
                        (forward_max, backward_max, -BIG, ALU.add, ALU.max, pen_row),
                        (forward_sum, backward_sum, 0.0, ALU.mult, ALU.add, joined))):
                    if kind == 1:
                        dve.wait_ge(powers_ready, 1)
                    for h in range(H):
                        forward(h, ident_f)
                        link(dve.tensor_copy(col[:, h:h + 1], fwd[:, T - 1:T]))
                    chained(0, masks[:, 0, :], ident_f, op0, op1)
                    link(dve.tensor_copy(carry_f[:, kind, :], carry[:]))
                    for h in range(H):
                        forward(h, carry_f[:, kind, h:h + 1])
                        backward(h, ident_f)
                        link(dve.tensor_copy(col[:, h:h + 1], bwd[:, 0:1]))
                    chained(1, masks[:, 1, :], ident_f, op0, op1)
                    for h in range(H):
                        forward(h, carry_f[:, kind, h:h + 1])
                        backward(h, carry[:, h:h + 1])
                        if kind == 0:
                            link(dve.tensor_tensor(scores[:, :, h], scores[:, :, h], bwd[:], ALU.subtract))
                        else:
                            link(dve.tensor_scalar(bwd[:], bwd[:], 1e-8, None, ALU.add))
                            link(dve.reciprocal(tmp[:], bwd[:]))
                            link(dve.tensor_tensor(tmp[:], powers[:, :, h], tmp[:], ALU.mult))
                            if h == 0:
                                link(dve.tensor_copy(weight[:], tmp[:]))
                            else:
                                link(dve.tensor_tensor(weight[:], weight[:], tmp[:], ALU.add))
                    if kind == 0:
                        dve.sem_inc(less_max, 1)
                dve.tensor_scalar(weight[:], weight[:], 1.0 / H, None, ALU.mult).then_inc(weight_ready, 1)

            @block.scalar
            def _(act):
                act.wait_ge(less_max, 1)
                act.activation(powers[:], scores, ACT.Exp).then_inc(powers_ready, 1)

            @block.tensor
            def _(pe):
                pe.wait_ge(ends_ready, 1)
                pe.transpose(psR[:, 0, :], ends[:, 0, :], z.ident[:])
                pe.transpose(psR[:, 1, :], ends[:, 1, :], z.ident[:]).then_inc(rows_ready, 1)
                pe.wait_ge(shifted, 1)
                pe.transpose(psC[:, 0, :], key_rows[:, 0, 0:P], z.ident[0:H, 0:H])
                pe.transpose(psC[:, 1, :], key_rows[:, 1, 1:P + 1], z.ident[0:H, 0:H]).then_inc(cols_ready, 1)
                for n in range(CHAINS):
                    pe.wait_ge(col_ready, n + 1)
                    pe.transpose(psr[:], col[:], z.ident[:]).then_inc(row_ready, 1)
                    pe.wait_ge(chain_ready, n + 1)
                    shown = chain[:, 0:P] if n % 2 == 0 else chain[:, 1:P + 1]
                    pe.transpose(psc[:], shown, z.ident[0:H, 0:H]).then_inc(carry_ready, 1)

            @block.sync
            def _(sp):
                sp.dma_start(edges[:], sorted_edges.rearrange("(p j) k -> p j k", p=P)).then_inc(edges_in, 16)
                sp.wait_ge(weight_ready, 1)
                for array, held in zip(flat, (src, dst, weight)):
                    sp.dma_start(array.rearrange("(p j) -> p j", p=P), held[:]).then_inc(flat_out, 16)
                sp.wait_ge(flat_out, 48)


def load_sorted(nc, z, flat, keyF, indexI, weightF):
    T, K = z.T, z.K
    fk, fr = T // P, T % P
    with ExitStack() as ctx:
        m = Mem(nc, ctx, "load_sorted")
        rows = [m.sb(f"rows{i}", [P, K, P]) for i in range(3)]
        index_f = m.sb("index_f", [P, T])
        turned = [m.psum(f"turned{i}", [P, 4 * 512]) for i in range(2)]
        rows_in, rows_turned, lists_out = m.sem("rows_in"), m.sem("rows_turned"), m.sem("lists_out")
        with nc.Block() as block:
            @block.sync
            def _(sp):
                for array, r in zip(flat, rows):
                    sp.dma_start(r[:, 0:fk, :], array[0:fk * P * P].rearrange("(k r c) -> r k c", r=P, c=P)
                                 ).then_inc(rows_in, 16)
                    sp.dma_start(r[0:fr, fk, :], array[fk * P * P:T * P].rearrange("(r c) -> r c", c=P)
                                 ).then_inc(rows_in, 16)

            @block.vector
            def _(dve):
                for i, out in enumerate((keyF, index_f, weightF)):
                    dve.wait_ge(rows_turned, i + 1)
                    for b in range(0, T, 512):
                        n = min(512, T - b)
                        ins = dve.tensor_copy(out[:, b:b + n], turned[i % 2][:, b:b + n])
                    ins.then_inc(lists_out, 1)
                dve.wait_ge(lists_out, 3)
                dve.tensor_copy(indexI[:], index_f[:])

            @block.tensor
            def _(pe):
                pe.wait_ge(rows_in, 6 * 16)
                for i in range(3):
                    if i == 2:
                        pe.wait_ge(lists_out, 1)
                    for k in range(K):
                        n = min(P, T - k * P)
                        ins = pe.transpose(turned[i % 2][:, k * P:k * P + n], rows[i][0:n, k, :], z.ident[0:n, 0:n])
                    ins.then_inc(rows_turned, 1)


def program(nc, x, src, dst, weight, w1, b1, g1, be1, w2, b2, g2, be2,
            sw1l, sb1, sw1r, sw2l, sb2, sw2r, wq, wk, wo, bo, gw, gb, out):
    z = Sizes(x.shape[0], src.shape[0])
    with ExitStack() as ctx:
        persist = Mem(nc, ctx, "kept")

        def dram(name, shape, dt=F32):
            return nc.dram_tensor(name, shape, dt, kind="Internal").ap()

        tabA, tabB, tabH, tabH2, tabV, tabX = (dram(n, (z.NP, C)) for n in ("tabA", "tabB", "tabH", "tabH2", "tabV", "tabX"))
        tabQ, tabK = dram("tabQ", (z.NP, 4)), dram("tabK", (z.NP, 4))
        tabQsum, sorted_edges = dram("tabQsum", (z.NP, 4)), dram("sorted_edges", (z.EP, 6))
        flat = [dram(n, (z.EP,)) for n in ("sorted_src", "sorted_dst", "sorted_weight")]
        make_constants(nc, z, persist)
        load_edge_lists(nc, z, persist, src, dst, weight)
        z.dst_tiles = find_tiles(nc, z, persist, z.dstF, "dst")
        z.X = persist.sb("X", [P, z.A, C])
        z.SUMX = persist.sb("SUMX", [P, z.A, 2])
        z.rcount = persist.sb("rcount", [P, z.A])
        z.dinv = persist.sb("dinv", [P, z.A])
        with ExitStack() as part:
            held = Mem(nc, part, "first")
            z.H = held.sb("H", [P, z.A, C])
            z.SUM = held.sb("SUM", [P, z.A, C])
            entry(nc, z, x, tabA, tabB, w1, b1)
            edge_mlp(nc, z, tabA, tabB, z.dst_tiles, w2, b2, g1, be1, g2, be2)
            after_mlp(nc, z, tabH)
            segment_sum(nc, z, "sum_sage1", z.dst_tiles, z.dstF, z.SUM, gather=(tabH, z.srcI), extras=z.one_w,
                        extras_out=z.SUMX)
            sage_layer(nc, z, "sage1", sw1l, sb1, sw1r, hidden_table=tabH2)
            segment_sum(nc, z, "sum_sage2", z.dst_tiles, z.dstF, z.SUM, gather=(tabH2, z.srcI))
            sage_layer(nc, z, "sage2", sw2l, sb2, sw2r, attention=(wq, wk, wo, bo, tabQ, tabK, tabV))
        with ExitStack() as part:
            held = Mem(nc, part, "sorting")
            z.srcHigh, z.srcLow = held.sb("srcHigh", [P, z.T]), held.sb("srcLow", [P, z.T])
            z.first = held.sb("first_rank", [P, z.A])
            query_sums(nc, z, tabQ, tabQsum)
            sort_and_score(nc, z, tabK, tabQsum, sorted_edges)
        edge_softmax(nc, z, sorted_edges, flat)
        with ExitStack() as part:
            held = Mem(nc, part, "second")
            z.H = held.sb("H", [P, z.A, C])
            z.SUM = held.sb("SUM", [P, z.A, C])
            with ExitStack() as inner:
                lists = Mem(nc, inner, "by_source")
                keyF, weightF = lists.sb("keyF", [P, z.T]), lists.sb("weightF", [P, z.T])
                indexI = lists.sb("indexI", [P, z.T], I32)
                load_sorted(nc, z, flat, keyF, indexI, weightF)
                src_tiles = find_tiles(nc, z, lists, keyF, "src")
                segment_sum(nc, z, "sum_attention", src_tiles, keyF, z.SUM, gather=(tabV, indexI), scale=weightF)
            after_attention(nc, z, tabX, gw)
            segment_sum(nc, z, "sum_gcn", z.dst_tiles, z.dstF, z.SUM, gather=(tabX, z.srcI),
                        scale=z.one_w[:, :, 1])
            finish(nc, z, out, gb)


_INS = (["x", "src", "dst", "edge_weight"] + ["L0_gnn_" + k for k in ("w1", "b1", "g1", "be1", "w2", "b2", "g2", "be2")]
        + ["L1_gnn_" + k for k in ("W1_l", "b1_l", "W1_r", "W2_l", "b2_l", "W2_r")]
        + ["L2_gnn_" + k for k in ("Wq", "Wk", "Wl", "bl")] + ["L3_gnn_W", "L3_gnn_b"])


def kernel(**inputs):
    import numpy as _np
    import concourse.bacc as _bacc
    from concourse import mybir as _mybir
    from concourse.bass_utils import run_bass_kernel_spmd as _run

    nc = _bacc.Bacc("TRN2", target_bir_lowering=False, num_devices=1)
    arrays, args = {}, []
    for name in _INS:
        a = _np.ascontiguousarray(inputs[name])
        arrays[f"in_{name}_dram"] = a
        args.append(nc.dram_tensor(f"in_{name}_dram", a.shape, _mybir.dt.from_np(a.dtype), kind="ExternalInput").ap())
    out = nc.dram_tensor("out_0_dram", inputs["x"].shape, F32, kind="ExternalOutput").ap()
    program(nc, *args, out)
    r = _run(nc, [arrays], core_ids=[0])
    return r.results[0]["out_0_dram"]
```
